# Optimizing a Trainium2 kernel written in Bass

```python
import numpy as np
import jax
import jax.numpy as jnp

def _softmax(x, axis=-1):
    return jax.nn.softmax(x, axis=axis)

def _gelu(x):
    return jax.nn.gelu(x, approximate=True)

def _silu(x):
    return jax.nn.silu(x)

def _sigmoid(x):
    return jax.nn.sigmoid(x)

def _layernorm(x, axis=-1, eps=1e-05):
    m = jnp.mean(x, axis=axis, keepdims=True)
    v = jnp.var(x, axis=axis, keepdims=True)
    return (x - m) / jnp.sqrt(v + eps)

def _scatter_add(tgt, idx, src, axis=0):
    return tgt.at[idx].add(src)

def _segment_sum(src, seg, n):
    return jax.ops.segment_sum(src, seg, n)
kernel_name = 'mk_adaln_ffn_d1_seqx_r8_67c5cd'

def setup_inputs(seed: int=0):
    np.random.seed(seed)
    _w = jnp.asarray

    def _rec_inputs():
        import jax
        import jax.numpy as jnp
        _rk = jax.random.key(seed)
        x = -0.0003929 + 0.9999 * jax.random.normal(jax.random.fold_in(_rk, 1), (64, 32, 512), jnp.float32)
        _lenS = 32 - jax.random.randint(jax.random.fold_in(_rk, 7), (64,), 0, max(1, 32 // 4) + 1, jnp.int32)
        _lenS2 = 32 - jax.random.randint(jax.random.fold_in(_rk, 8), (64,), 0, max(1, 32 // 4) + 1, jnp.int32)
        cond_512 = 0.00782532 + 1.00527 * jax.random.normal(jax.random.fold_in(_rk, 11), (64, 64), jnp.float32)
        return (x, cond_512)
    x, cond_512 = _rec_inputs()

    def _L0_cond_setup():
        import jax, jax.numpy as jnp
        from jax import lax
        import numpy as np
        CIN, COUT, K, STYLE_DIM = (32, 32, 3, 64)
        N_LAYERS = 4
        TYPES = ('same', 'upsample', 'same', 'downsample')
        SCALE = 1.0 / float(np.sqrt(CIN * K ** 2))
        EPS = 1e-08
        _BK = np.array([1.0, 3.0, 3.0, 1.0], dtype=np.float32)
        BLUR_K = _BK / _BK.sum()

        def _blur(x, kern, pad):
            B, C, _ = x.shape
            xp = jnp.pad(x, ((0, 0), (0, 0), (pad[0], pad[1])))
            w = jnp.broadcast_to(kern.astype(x.dtype)[None, None, :], (C, 1, kern.shape[0]))
            return lax.conv_general_dilated(xp, w, (1,), 'VALID', feature_group_count=C, dimension_numbers=('NCH', 'OIH', 'NCH'))

        def _conv_same(x, w):
            p = (K - 1) // 2
            return lax.conv_general_dilated(x[None], w, (1,), [(p, p)], dimension_numbers=('NCH', 'OIH', 'NCH'))[0]

        def _conv_down(x, w):
            return lax.conv_general_dilated(x[None], w, (2,), 'VALID', dimension_numbers=('NCH', 'OIH', 'NCH'))[0]

        def _conv_up(x, w_t):
            return lax.conv_transpose(x[None], w_t, (2,), 'VALID', dimension_numbers=('NCH', 'IOH', 'NCH'), transpose_kernel=True)[0]

        def _layer(x, style, w, b, mw, mb, typ):
            s = style @ mw.T + mb
            weight = SCALE * w * s[:, None, :, None]
            demod = lax.rsqrt(jnp.sum(weight * weight, axis=(2, 3)) + EPS)
            weight = weight * demod[:, :, None, None]
            blur_k = jnp.asarray(BLUR_K)
            if typ == 'same':
                out = jax.vmap(_conv_same)(x, weight) + b[None, :, None]
            elif typ == 'upsample':
                out = jax.vmap(_conv_up)(x, weight.transpose(0, 2, 1, 3)) + b[None, :, None]
                out = _blur(out, 2.0 * blur_k, (1, 1))
            elif typ == 'downsample':
                xb = _blur(x, blur_k, (2, 2))
                out = jax.vmap(_conv_down)(xb, weight) + b[None, :, None]
            else:
                raise NotImplementedError(typ)
            return out
        key = jax.random.key(seed)
        ks = jax.random.split(key, 6)
        B, L = (16, 512)
        return {'x': jax.random.normal(ks[0], (B, CIN, L), dtype=jnp.float32), 'style': jax.random.normal(ks[1], (B, STYLE_DIM), dtype=jnp.float32), 'weights': jax.random.normal(ks[2], (N_LAYERS, COUT, CIN, K), dtype=jnp.float32), 'biases': jax.random.normal(ks[3], (N_LAYERS, COUT), dtype=jnp.float32) * 0.1, 'mod_w': jax.random.normal(ks[4], (N_LAYERS, CIN, STYLE_DIM), dtype=jnp.float32) / np.sqrt(STYLE_DIM), 'mod_b': 1.0 + 0.1 * jax.random.normal(ks[5], (N_LAYERS, CIN), dtype=jnp.float32)}
    _L0_cond_all = _L0_cond_setup()
    _L0_cond_in = {k: v for k, v in _L0_cond_all.items() if k in ('weights', 'biases', 'mod_w', 'mod_b')}
    del _L0_cond_all

    def _L0_ffn_setup():
        import jax, jax.numpy as jnp
        import numpy as np
        B_, S, D_IN, D_OUT = (4, 256, 512, 512)
        N, RANK, ALPHA = (8, 16, 32)
        SCALE = ALPHA / RANK
        key = jax.random.key(seed)
        kx, ka, kb, kw, kbias = jax.random.split(key, 5)
        x = jax.random.normal(kx, (B_, S, D_IN), dtype=jnp.float32)
        lora_A = jax.random.normal(ka, (N, RANK, D_IN), dtype=jnp.float32) * (1.0 / np.sqrt(D_IN))
        lora_B = jax.random.normal(kb, (N, D_OUT, RANK), dtype=jnp.float32) * (1.0 / np.sqrt(RANK))
        W = jax.random.normal(kw, (D_OUT, D_IN), dtype=jnp.float32) * (1.0 / np.sqrt(D_IN))
        bias = jax.random.normal(kbias, (D_OUT,), dtype=jnp.float32) * 0.01
        lora_weights = jnp.full((N,), 1.0 / N, dtype=jnp.float32)
        return {'x': x, 'lora_A': lora_A, 'lora_B': lora_B, 'W': W, 'bias': bias, 'lora_weights': lora_weights}
    _L0_ffn_all = _L0_ffn_setup()
    _L0_ffn_in = {k: v for k, v in _L0_ffn_all.items() if k in ('lora_A', 'lora_B', 'W', 'bias', 'lora_weights')}
    del _L0_ffn_all
    return {'x': x, 'cond_512': cond_512, 'L0_cond_weights': _L0_cond_in['weights'], 'L0_cond_biases': _L0_cond_in['biases'], 'L0_cond_mod_w': _L0_cond_in['mod_w'], 'L0_cond_mod_b': _L0_cond_in['mod_b'], 'L0_ffn_lora_A': _L0_ffn_in['lora_A'], 'L0_ffn_lora_B': _L0_ffn_in['lora_B'], 'L0_ffn_W': _L0_ffn_in['W'], 'L0_ffn_bias': _L0_ffn_in['bias'], 'L0_ffn_lora_weights': _L0_ffn_in['lora_weights']}

def reference(x, cond_512, L0_cond_weights, L0_cond_biases, L0_cond_mod_w, L0_cond_mod_b, L0_ffn_lora_A, L0_ffn_lora_B, L0_ffn_W, L0_ffn_bias, L0_ffn_lora_weights):
    import jax
    import jax.numpy as jnp

    def _L0_cond_ref(x, style, weights, biases, mod_w, mod_b):
        import jax, jax.numpy as jnp
        from jax import lax
        import numpy as np
        CIN, COUT, K, STYLE_DIM = (32, 32, 3, 64)
        N_LAYERS = 4
        TYPES = ('same', 'upsample', 'same', 'downsample')
        SCALE = 1.0 / float(np.sqrt(CIN * K ** 2))
        EPS = 1e-08
        _BK = np.array([1.0, 3.0, 3.0, 1.0], dtype=np.float32)
        BLUR_K = _BK / _BK.sum()

        def _blur(x, kern, pad):
            B, C, _ = x.shape
            xp = jnp.pad(x, ((0, 0), (0, 0), (pad[0], pad[1])))
            w = jnp.broadcast_to(kern.astype(x.dtype)[None, None, :], (C, 1, kern.shape[0]))
            return lax.conv_general_dilated(xp, w, (1,), 'VALID', feature_group_count=C, dimension_numbers=('NCH', 'OIH', 'NCH'))

        def _conv_same(x, w):
            p = (K - 1) // 2
            return lax.conv_general_dilated(x[None], w, (1,), [(p, p)], dimension_numbers=('NCH', 'OIH', 'NCH'))[0]

        def _conv_down(x, w):
            return lax.conv_general_dilated(x[None], w, (2,), 'VALID', dimension_numbers=('NCH', 'OIH', 'NCH'))[0]

        def _conv_up(x, w_t):
            return lax.conv_transpose(x[None], w_t, (2,), 'VALID', dimension_numbers=('NCH', 'IOH', 'NCH'), transpose_kernel=True)[0]

        def _layer(x, style, w, b, mw, mb, typ):
            s = style @ mw.T + mb
            weight = SCALE * w * s[:, None, :, None]
            demod = lax.rsqrt(jnp.sum(weight * weight, axis=(2, 3)) + EPS)
            weight = weight * demod[:, :, None, None]
            blur_k = jnp.asarray(BLUR_K)
            if typ == 'same':
                out = jax.vmap(_conv_same)(x, weight) + b[None, :, None]
            elif typ == 'upsample':
                out = jax.vmap(_conv_up)(x, weight.transpose(0, 2, 1, 3)) + b[None, :, None]
                out = _blur(out, 2.0 * blur_k, (1, 1))
            elif typ == 'downsample':
                xb = _blur(x, blur_k, (2, 2))
                out = jax.vmap(_conv_down)(xb, weight) + b[None, :, None]
            else:
                raise NotImplementedError(typ)
            return out
        out = x
        for i, typ in enumerate(TYPES):
            out = _layer(out, style, weights[i], biases[i], mod_w[i], mod_b[i], typ)
        return out

    def _L0_ffn_ref(x, lora_A, lora_B, W, bias, lora_weights):
        import jax, jax.numpy as jnp
        import numpy as np
        B_, S, D_IN, D_OUT = (4, 256, 512, 512)
        N, RANK, ALPHA = (8, 16, 32)
        SCALE = ALPHA / RANK
        h = jnp.einsum('bsd,nrd->nbsr', x, lora_A)
        coef = (SCALE * lora_weights)[:, None, None]
        lora_out = jnp.einsum('nbsr,nor->bso', h, lora_B * coef)
        base = jnp.einsum('bsd,od->bso', x, W) + bias
        return base + lora_out
    x = x + _L0_ffn_ref(_L0_cond_ref(x, cond_512, L0_cond_weights, L0_cond_biases, L0_cond_mod_w, L0_cond_mod_b), L0_ffn_lora_A, L0_ffn_lora_B, L0_ffn_W, L0_ffn_bias, L0_ffn_lora_weights)
    return x

_drawn_inputs = setup_inputs


def setup_inputs(seed=0):
    import zlib

    import numpy as np

    out = dict(_drawn_inputs(seed))
    spreads = {'L0_ffn_lora_weights': (0.125, 0.2)}
    factors = {'L0_ffn_bias': 7.827}
    for name, (base, spread) in spreads.items():
        noise = np.random.default_rng([zlib.crc32(name.encode()), seed]).standard_normal(out[name].shape)
        drawn = base * np.exp(spread * noise) if base else spread * noise
        out[name] = jnp.asarray(drawn.astype(out[name].dtype))
    for name, factor in factors.items():
        out[name] = (out[name] * factor).astype(out[name].dtype)
    return out
```

```python
from contextlib import ExitStack

import numpy as np

import concourse.bass as bass
from concourse import mybir

F32 = mybir.dt.float32
ALU = mybir.AluOpType
ACT = mybir.ActivationFunctionType

B, C, L = 64, 32, 512
LAYERS, K, STYLE = 4, 3, 64
RANKS = 128
P = 128
POS = P // C
J = L // POS
OCT = 8
QUAD = 4
NOCT = B // OCT
HALVES = OCT // QUAD
TAPS = 6
SCALE = 1.0 / float(np.sqrt(C * K ** 2))
LORA_SCALE = 32 / 16
EPS = 1e-8
BLUR = [1 / 8, 3 / 8, 3 / 8, 1 / 8]
W0T, W0F, W1F, W1T, W2T, W2F, W3F = range(7)


def build(nc, wpack, style, cols, lora_a, lora_b, wt, bias, x_blocks, x_edges, x_rows, out):
    ctx = ExitStack()
    with ctx:
        def sb(name, shape):
            return ctx.enter_context(nc.sbuf_tensor(name, shape, F32))

        def pb(name, shape):
            return ctx.enter_context(nc.psum_tensor(name, shape, F32))

        def sem(name):
            return ctx.enter_context(nc.semaphore(name))

        w_sb = sb("w_sb", [P, 7, K * C])
        style_sb = sb("style_sb", [STYLE, LAYERS * P + B])
        cols_sb = sb("cols_sb", [P, 9])
        lora_a_sb = sb("lora_a_sb", [P, J, POS])
        lora_b_sb = sb("lora_b_sb", [P, L])
        w_eff = sb("w_eff", [P, POS, L])
        bias_sb = sb("bias_sb", [P, L])
        x_edge = sb("x_edge", [P, 4, B])
        x_half = [sb(f"x_half{h}", [P, QUAD, J + 2]) for h in range(HALVES)]
        blur1 = sb("blur1", [P, TAPS * C])
        blur1r = sb("blur1r", [P, TAPS * C])
        blur3r = sb("blur3r", [P, TAPS * C])
        s0t = sb("s0t", [P, 8 * C])
        s2t = sb("s2t", [P, 6 * C])
        s1t = sb("s1t", [P, 10 * C])
        s0f = sb("s0f", [P, 12 * C])
        s2f = sb("s2f", [P, 12 * C])
        s1f = sb("s1f", [P, 16 * C])
        s3f = sb("s3f", [P, 10 * C])
        w3_taps = sb("w3_taps", [P, 2, C])
        sty = sb("sty", [P, LAYERS, B])
        sty2 = sb("sty2", [P, LAYERS, B])
        dem = sb("dem", [P, LAYERS, B])
        root = sb("root", [P, LAYERS, B])
        eps_col = sb("eps_col", [P, 1])
        wsq = sb("wsq", [C, LAYERS, K, C])
        wsum2 = sb("wsum2", [C, LAYERS, C])
        wsum2r = sb("wsum2r", [C, LAYERS, POS, C])
        sc_t = sb("sc_t", [P, B])
        sc_v = sb("sc_v", [P, 3, B])
        sc_y0 = sb("sc_y0", [P, B])
        sc_t3 = sb("sc_t3", [P, 3, B])
        bs_y0 = sb("bs_y0", [P, B])
        bs_v = sb("bs_v", [P, 3, B])
        bs_t = sb("bs_t", [P, 3, B])
        bs_end = sb("bs_end", [P, B])
        out_scale = sb("out_scale", [P, B // QUAD])
        out_const = sb("out_const", [P, B // QUAD])
        const_rep = sb("const_rep", [P, B])
        a_t = sb("a_t", [P, 2, OCT, C])
        a_v = sb("a_v", [P, 2, OCT, C])
        a_y0 = sb("a_y0", [P, 2, OCT, C])
        taps = sb("taps", [P, 3, POS, OCT, C])
        e_x = sb("e_x", [P, 4, B])
        e_y0 = sb("e_y0", [P, 3, 3 * B])
        e_v = sb("e_v", [P, 8 * B])
        e_t = sb("e_t", [P, 8 * B])
        e_c = sb("e_c", [B, P])
        e_out = sb("e_out", [B, 2, P])
        y_half = [sb(f"y_half{h}", [P, POS, QUAD, C]) for h in range(HALVES)]
        r_half = [sb(f"r_half{h}", [P, L]) for h in range(HALVES)]
        o_half = [sb(f"o_half{h}", [P, L]) for h in range(HALVES)]
        coef = sb("coef", [P, 1])
        lora_bc = sb("lora_bc", [P, L])
        w_part = sb("w_part", [P, 2, L])
        w_fold = sb("w_fold", [P, L])
        w_total = sb("w_total", [P, L])
        ones = sb("ones", [P, P])

        ps_y = [pb(f"ps_y{h}", [P, L]) for h in range(HALVES)]
        ps_z = [pb(f"ps_z{h}", [P, L]) for h in range(HALVES)]
        ps_av = pb("ps_av", [P, L])
        ps_ay0 = pb("ps_ay0", [P, L])
        ps_h = pb("ps_h", [P, L])
        ps_h4 = pb("ps_h4", [P, L])

        e_dram = nc.dram_tensor("edge_rows", [2, POS, B, C], F32, kind="Internal").ap()

        ld_style = sem("ld_style")
        ld_cols = sem("ld_cols")
        ld_w = sem("ld_w")
        ld_xe = sem("ld_xe")
        ld_wt = sem("ld_wt")
        ld_lora_a = sem("ld_lora_a")
        ld_lora_b = sem("ld_lora_b")
        ld_bias = sem("ld_bias")
        ld_x = [sem(f"ld_x{h}") for h in range(HALVES)]
        ld_r = [sem(f"ld_r{h}") for h in range(HALVES)]
        zeroed = sem("zeroed")
        strip_t = sem("strip_t")
        strip_f = sem("strip_f")
        ve = sem("ve")
        sty2_ready = sem("sty2_ready")
        lora_added = sem("lora_added")
        wtot_copied = sem("wtot_copied")
        sty_mm = sem("sty_mm")
        dem_mm = sem("dem_mm")
        rooted = sem("rooted")
        lora_mm = sem("lora_mm")
        wtot_mm = sem("wtot_mm")
        edge_mm = sem("edge_mm")
        edge_written = sem("edge_written")
        e_in = sem("e_in")
        e_stage = sem("e_stage")
        lora_ready = sem("lora_ready")
        wfold_ready = sem("wfold_ready")
        e_rows = sem("e_rows")
        at_ready = sem("at_ready")
        av_mm = sem("av_mm")
        av_ready = sem("av_ready")
        ay0_mm = sem("ay0_mm")
        ay0_ready = sem("ay0_ready")
        h_mm = sem("h_mm")
        h_ready = sem("h_ready")
        taps_in = sem("taps_in")
        taps_in2 = sem("taps_in2")
        conv_mm = [sem(f"conv_mm{h}") for h in range(HALVES)]
        y_ready = [sem(f"y_ready{h}") for h in range(HALVES)]
        ends_in = [sem(f"ends_in{h}") for h in range(HALVES)]
        z_mm = [sem(f"z_mm{h}") for h in range(HALVES)]
        r_biased = [sem(f"r_biased{h}") for h in range(HALVES)]
        r_const = [sem(f"r_const{h}") for h in range(HALVES)]
        o_ready = [sem(f"o_ready{h}") for h in range(HALVES)]
        stored = [sem(f"stored{h}") for h in range(HALVES)]

        block = ctx.enter_context(nc.Block())

        LEFT, CONST, RIGHT = slice(0, B), slice(B, 2 * B), slice(2 * B, 3 * B)
        ALL, LEFT_CONST, CONST_RIGHT = slice(0, 3 * B), slice(0, 2 * B), slice(B, 3 * B)

        def window(strip, first, n=POS):
            return strip[:, first * C:(first + n) * C]

        def over_c(t, n=C):
            return t.unsqueeze(2).broadcast_to([P, OCT, n])

        @block.sync
        def _(sp):
            sp.dma_start(style_sb[:, :], style).then_inc(ld_style, 16)
            sp.dma_start(w_sb[:, :, :].rearrange("p k f -> p (k f)"), wpack).then_inc(ld_w, 16)
            sp.dma_start(x_edge[:, :, :], x_edges).then_inc(ld_xe, 16)
            sp.wait_ge(zeroed, 1)
            for h in range(HALVES):
                sp.dma_start(x_half[h][:, :, 1:1 + J], x_blocks[:, h * QUAD:(h + 1) * QUAD, :]).then_inc(ld_x[h], 16)
            for h in range(HALVES):
                sp.dma_start(r_half[h][:, :], x_rows[h * P:(h + 1) * P, :]).then_inc(ld_r[h], 16)

            def shift_taps(n):
                sp.wait_ge(h_ready, n + 1)
                for q in range(1, POS):
                    sp.dma_start(taps[q * C:P, :, q, :, :], taps[0:P - q * C, :, 0, :, :]).then_inc(taps_in, 16)
                    sp.dma_start(taps[0:q * C, 1:3, q, :, :], taps[P - q * C:P, 0:2, 0, :, :]).then_inc(taps_in2, 16)

            shift_taps(0)
            sp.wait_ge(e_rows, 1)
            for side in range(2):
                sp.dma_start(e_dram[side].rearrange("q b c -> b q c"),
                             e_out[:, side, :].rearrange("b (q c) -> b q c", q=POS)).then_inc(edge_written, 16)

            def octet(i, last):
                if not last:
                    for h in range(HALVES):
                        sp.wait_ge(conv_mm[h], i + 1)
                        sp.dma_start(x_half[h][:, :, 1:1 + J],
                                     x_blocks[:, bass.ds((i + 1) * OCT + h * QUAD, QUAD), :]).then_inc(ld_x[h], 16)
                    shift_taps(i + 1)
                for h in range(HALVES):
                    sp.wait_ge(o_ready[h], i + 1)
                    sp.dma_start(out[bass.ds((i * HALVES + h) * P, P), :], o_half[h][:, :]).then_inc(stored[h], 16)
                    if not last:
                        sp.dma_start(r_half[h][:, :],
                                     x_rows[bass.ds(((i + 1) * HALVES + h) * P, P), :]).then_inc(ld_r[h], 16)

            with sp.Fori(0, NOCT - 1) as i:
                octet(i, False)
            octet(NOCT - 1, True)
            for h in range(HALVES):
                sp.wait_ge(stored[h], 16 * NOCT)

        @block.gpsimd
        def _(pool):
            for h in range(HALVES):
                nc.gpsimd.memset(x_half[h][:, :, 0:J + 2:J + 1], 0.0)
            for s in (s2t, s1t, s0t, s3f, s0f, s2f):
                nc.gpsimd.memset(s[:, :], 0.0)
            nc.gpsimd.memset(s1f[:, :], 0.0)
            nc.gpsimd.memset(taps[:, 2, 0, :, :], 0.0)
            nc.gpsimd.memset(taps[:, 0, :, :, :], 0.0)
            nc.gpsimd.memset(eps_col[:, :], EPS)
            nc.gpsimd.memset(ones[:, :], 1.0).then_inc(zeroed, 1)
            pool.wait_ge(zeroed, 1)
            pool.wait_ge(ld_w, 16)
            for strip, kind in ((s2t, W2T), (s0t, W0T)):
                for p in range(POS):
                    q = slice(p * C, (p + 1) * C)
                    nc.gpsimd.tensor_copy(strip[q, p * C:(p + K) * C], w_sb[q, kind, :]).then_inc(strip_t, 1)
            pool.wait_ge(strip_t, 2 * POS)
            pool.wait_ge(ld_bias, 16)

            def octet(i):
                for h in range(HALVES):
                    pool.wait_ge(ld_r[h], 16 * (i + 1))
                    nc.gpsimd.tensor_tensor(r_half[h][:, :], r_half[h][:, :], bias_sb[:, :],
                                            ALU.add).then_inc(r_biased[h], 1)
                    pool.wait_ge(r_biased[h], i + 1)

            with pool.Fori(0, NOCT) as i:
                octet(i)

        @block.scalar
        def _(act):
            act.dma_start(cols_sb[:, :], cols).then_inc(ld_cols, 16)
            act.dma_start(w_eff[:, :, :].rearrange("p q o -> p (q o)"), wt).then_inc(ld_wt, 16)
            act.dma_start(lora_a_sb[:, :, :].rearrange("r j q -> r (j q)"), lora_a).then_inc(ld_lora_a, 16)
            act.dma_start(lora_b_sb[:, :], lora_b).then_inc(ld_lora_b, 16)
            act.dma_start(bias_sb[:, :], bias.broadcast_to([P, L])).then_inc(ld_bias, 16)
            act.wait_ge(ld_w, 16)
            act.wait_ge(zeroed, 1)
            act.wait_ge(dem_mm, 1)
            nc.scalar.activation(root[:, :, :].rearrange("p l b -> p (l b)"), ps_z[1][:, 0:LAYERS * B],
                                 ACT.Sqrt, bias=eps_col[:, :]).then_inc(rooted, 1)
            for strip, kind in ((s0f, W0F), (s2f, W2F)):
                for p in range(POS):
                    q = slice(p * C, (p + 1) * C)
                    nc.scalar.activation(strip[q, (p + 3) * C:(p + 6) * C], w_sb[q, kind, :],
                                         ACT.Copy).then_inc(strip_f, 1)

            def octet(i):
                for h in range(HALVES):
                    act.wait_ge(conv_mm[h], i + 1)
                    if not isinstance(i, int):
                        act.wait_ge(z_mm[h], i)
                    nc.scalar.activation(y_half[h][:, :, :, :].rearrange("j q b c -> j b q c"),
                                         ps_y[h][:, :].rearrange("j (b q c) -> j b q c", b=QUAD, q=POS),
                                         ACT.Copy).then_inc(y_ready[h], 1)
                    if isinstance(i, int):
                        act.wait_ge(edge_written, 32)
                    act.wait_ge(y_ready[h], i + 1)
                    act.dma_start(y_half[h][0:P:P - 1, :, :, :],
                                  e_dram[:, :, bass.ds(i * OCT + h * QUAD, QUAD), :]
                                  ).then_inc(ends_in[h], 16)

            octet(0)
            with act.Fori(1, NOCT) as i:
                octet(i)

        @block.vector
        def _(dve):
            done = [0]

            def link(ins):
                done[0] += 1
                ins.then_inc(ve, 1)
                dve.wait_ge(ve, done[0])

            V = nc.vector
            dve.wait_ge(ld_w, 16)
            for l, kind in enumerate((W0F, W1T, W2F, W3F)):
                last = V.tensor_tensor(wsq[:, l, :, :].rearrange("p k c -> p (k c)"),
                                       w_sb[0:C, kind, :], w_sb[0:C, kind, :], ALU.mult)
            link(last)
            link(V.tensor_tensor(wsum2[:, :, :], wsq[:, :, 0, :], wsq[:, :, 1, :], ALU.add))
            link(V.tensor_tensor(wsum2[:, :, :], wsum2[:, :, :], wsq[:, :, 2, :], ALU.add))
            for p in range(POS):
                last = V.tensor_copy(wsum2r[:, :, p, :], wsum2[:, :, :])
            link(last)
            for dst, kind, gain in ((blur3r, W3F, 1.0), (blur1r, W1T, 2.0), (blur1, W1F, 2.0)):
                last = V.memset(dst[:, :], 0.0)
            link(last)
            dve.wait_ge(sty_mm, 1)
            dve.wait_ge(ld_cols, 16)
            for l in range(LAYERS):
                last = V.tensor_scalar(sty[:, l, :], ps_z[0][:, l * B:(l + 1) * B], cols_sb[:, l:l + 1], SCALE,
                                       ALU.add, ALU.mult)
            link(last)
            V.tensor_tensor(sty2[:, :, :], sty[:, :, :], sty[:, :, :], ALU.mult).then_inc(sty2_ready, 1)
            for j, tap in enumerate(BLUR):
                for dst, kind, gain in ((blur3r, W3F, 1.0), (blur1r, W1T, 2.0), (blur1, W1F, 2.0)):
                    part = dst[:, j * C:(j + K) * C]
                    last = V.scalar_tensor_tensor(part, w_sb[:, kind, :], gain * tap, part, ALU.mult, ALU.add)
                link(last)
            for p in range(POS):
                q = slice(p * C, (p + 1) * C)
                src = blur3r[q, :].rearrange("c (k o) -> c k o", o=C)[:, 3 - p:6 - p:2, :]
                last = V.tensor_copy(w3_taps[q, :, :], src)
            link(last)
            dve.wait_ge(rooted, 1)
            link(V.reciprocal(dem[:, :, :], root[:, :, :]))
            link(V.tensor_tensor(sc_t[:, :], dem[:, 2, :], sty[:, 3, :], ALU.mult))

            def start_taps(col):
                for slot in range(2):
                    last = V.tensor_tensor(a_t[:, slot, :, :],
                                           w3_taps[:, slot, :].unsqueeze(1).broadcast_to([P, OCT, C]),
                                           over_c(sc_t[:, col]), ALU.mult)
                last.then_inc(at_ready, 1)

            start_taps(slice(0, OCT))
            dve.wait_ge(zeroed, 1)
            for p in range(POS):
                q = slice(p * C, (p + 1) * C)
                view = blur1r[q, :].rearrange("c (k o) -> c k o", o=C)
                first = {0: -2, 1: -1, 2: -1, 3: 0}[p]
                k0 = 4 - p + 2 * first
                last = V.tensor_copy(s1t[q, (first + 4) * C:(first + 7) * C].rearrange("c (k o) -> c k o", o=C),
                                     view[:, k0:min(k0 + 5, TAPS):2, :])
            for k in range(3):
                last = V.tensor_tensor(sc_v[:, k, :], sty[:, 2, :], sty[:, 1, :], ALU.mult)
            last = V.tensor_tensor(sc_y0[:, :], dem[:, 1, :], dem[:, 0, :], ALU.mult)
            link(last)

            def scale_av(col):
                V.tensor_tensor(a_v[:, :, :, :], ps_av[:, :].rearrange("p (s b c) -> p s b c", s=2, b=OCT),
                                sc_v[:, 0, col].unsqueeze(1).unsqueeze(3).broadcast_to([P, 2, OCT, C]),
                                ALU.mult).then_inc(av_ready, 1)

            def scale_ay0(col):
                V.tensor_tensor(a_y0[:, :, :, :], ps_ay0[:, :].rearrange("p (s b c) -> p s b c", s=2, b=OCT),
                                sc_y0[:, col].unsqueeze(1).unsqueeze(3).broadcast_to([P, 2, OCT, C]),
                                ALU.mult).then_inc(ay0_ready, 1)

            def scale_h(col):
                V.tensor_tensor(taps[:, 0:2, 0, :, :], ps_h[:, :].rearrange("p (s b c) -> p s b c", s=2, b=OCT),
                                sty[:, 0, col].unsqueeze(1).unsqueeze(3).broadcast_to([P, 2, OCT, C]), ALU.mult)
                V.tensor_tensor(taps[0:C, 2, 0, :, :], ps_h4[0:C, 0:OCT * C].rearrange("p (b c) -> p b c", b=OCT),
                                sty[0:C, 0, col].unsqueeze(2).broadcast_to([C, OCT, C]),
                                ALU.mult).then_inc(h_ready, 1)

            dve.wait_ge(av_mm, 1)
            scale_av(slice(0, OCT))
            dve.wait_ge(ld_xe, 16)
            V.tensor_tensor(e_x[:, :, :], x_edge[:, :, :], sty[:, 0:1, :].broadcast_to([P, 4, B]), ALU.mult)
            V.tensor_scalar(bs_y0[:, :], dem[:, 1, :], cols_sb[:, 4:5], None, ALU.mult)
            V.tensor_scalar(bs_end[:, :], sty[:, 2, :], cols_sb[:, 5:6], -2.0 * BLUR[0], ALU.mult, ALU.mult)
            for k in range(3):
                V.tensor_scalar(bs_v[:, k, :], sty[:, 2, :], cols_sb[:, 5:6], 2.0, ALU.mult, ALU.mult)
                V.tensor_scalar(bs_t[:, k, :], sty[:, 3, :], cols_sb[:, 6:7], None, ALU.mult)
                V.tensor_copy(sc_t3[:, k, :], sc_t[:, :])
            V.tensor_scalar(coef[:, :], cols_sb[:, 8:9], LORA_SCALE, None, ALU.mult)
            for p in range(POS):
                q = slice(p * C, (p + 1) * C)
                V.tensor_copy(s1f[q, (2 * p + 2) * C:(2 * p + 8) * C], blur1[q, :])
                view = blur3r[q, :].rearrange("c (k o) -> c k o", o=C)
                first = p // 2 - 1
                k0 = 3 - p + 2 * first
                last = V.tensor_copy(s3f[q, (first + 4) * C:(first + 7) * C].rearrange("c (k o) -> c k o", o=C),
                                     view[:, k0:min(k0 + 5, TAPS):2, :])
            link(last)
            for k in range(3):
                last = V.tensor_copy(e_y0[:, k, CONST], bs_y0[:, :])
            last.then_inc(e_in, 1)
            dve.wait_ge(ay0_mm, 1)
            scale_ay0(slice(0, OCT))
            dve.wait_ge(ld_lora_b, 16)
            V.tensor_scalar(lora_bc[:, :], lora_b_sb[:, :], coef[:, 0:1], None, ALU.mult).then_inc(lora_ready, 1)

            dve.wait_ge(edge_mm, 1)
            for k, (blk, col) in enumerate(((0, RIGHT), (1, RIGHT), (1, LEFT), (2, LEFT))):
                last = V.tensor_tensor(e_y0[:, blk, col], ps_y[0][:, k * B:(k + 1) * B], sc_y0[:, :], ALU.mult)
            link(last)
            for k, (blk, col) in enumerate(((0, RIGHT), (1, RIGHT), (1, LEFT), (2, LEFT))):
                last = V.tensor_tensor(e_y0[:, blk, col], e_y0[:, blk, col], bs_y0[:, :], ALU.add)
            last.then_inc(e_stage, 1)
            dve.wait_ge(h_mm, 1)
            scale_h(slice(0, OCT))
            start_taps(slice(OCT, 2 * OCT))

            def end_stage(dst, src, scale, shift):
                for at, n in ((0, 3), (3, 3), (6, 2)):
                    part = slice(at * B, (at + n) * B)
                    last = V.tensor_tensor(dst[:, part], src[:, part],
                                           scale[:, 0:n, :].rearrange("p k b -> p (k b)"), ALU.mult)
                link(last)
                for at, n in ((0, 3), (3, 3), (6, 2)):
                    part = slice(at * B, (at + n) * B)
                    last = V.tensor_tensor(dst[:, part], dst[:, part],
                                           shift[:, 0:n, :].rearrange("p k b -> p (k b)"), ALU.add)
                return last

            dve.wait_ge(edge_mm, 2)
            link(end_stage(e_v, ps_y[1], sc_v, bs_v))
            V.tensor_tensor(e_v[0:C, 0:B], e_v[0:C, 0:B], bs_end[0:C, :], ALU.add)
            outer = slice(5 * B, 6 * B)
            V.tensor_tensor(e_v[P - C:P, outer], e_v[P - C:P, outer], bs_end[P - C:P, :],
                            ALU.add).then_inc(e_stage, 1)

            dve.wait_ge(ld_wt, 16)
            for q in range(POS):
                dve.wait_ge(lora_mm, q + 1)
                V.tensor_tensor(w_eff[:, q, :], w_eff[:, q, :], (ps_z[1], ps_ay0)[q % 2][:, :],
                                ALU.add).then_inc(lora_added, 1)

            dve.wait_ge(edge_mm, 3)
            end_stage(e_t, ps_z[0], sc_t3, bs_t).then_inc(e_stage, 1)
            dve.wait_ge(lora_added, POS)
            V.tensor_tensor(w_part[:, 0, :], w_eff[:, 0, :], w_eff[:, 1, :], ALU.add)
            link(V.tensor_tensor(w_part[:, 1, :], w_eff[:, 2, :], w_eff[:, 3, :], ALU.add))
            V.tensor_tensor(w_fold[:, :], w_part[:, 0, :], w_part[:, 1, :], ALU.add).then_inc(wfold_ready, 1)

            dve.wait_ge(edge_mm, 4)
            link(V.tensor_copy(e_c[:, :], ps_h4[0:B, 2 * P:3 * P]))
            for side in range(2):
                last = V.tensor_tensor(e_out[:, side, :], ps_h4[0:B, side * P:(side + 1) * P], e_c[:, :],
                                       ALU.subtract)
            last.then_inc(e_rows, 1)
            link(V.tensor_tensor(const_rep[:, :], ps_h4[:, 3 * P:3 * P + B], dem[:, 3, :], ALU.mult))
            for r in range(QUAD):
                q = slice(r * C, (r + 1) * C)
                V.tensor_copy(out_scale[q, :], dem[q, 3, r:B:QUAD])
                last = V.tensor_scalar(out_const[q, :], const_rep[q, r:B:QUAD], cols_sb[q, 7:8], None, ALU.add)
            link(last)
            dve.wait_ge(wtot_mm, 1)
            V.tensor_copy(w_total[:, :], ps_ay0[:, :]).then_inc(wtot_copied, 1)
            dve.wait_ge(wtot_copied, 1)

            def octet(i, walk=True, start=True):
                def col(n):
                    return slice(n * OCT, (n + 1) * OCT) if isinstance(n, int) else bass.ds(n * OCT, OCT)

                def row(t, h):
                    return t[:, bass.ds(i * HALVES + h, 1)]

                def add_const(h):
                    dve.wait_ge(r_biased[h], i + 1)
                    V.scalar_tensor_tensor(r_half[h][:, :], w_total[:, :], row(out_const, h), r_half[h][:, :],
                                           ALU.mult, ALU.add).then_inc(r_const[h], 1)

                if walk:
                    dve.wait_ge(av_mm, i + 2)
                    scale_av(col(i + 1))
                add_const(0)
                if walk:
                    dve.wait_ge(ay0_mm, i + 2)
                    scale_ay0(col(i + 1))
                add_const(1)
                if walk:
                    dve.wait_ge(h_mm, i + 2)
                    scale_h(col(i + 1))
                if start:
                    start_taps(col(i + 2))
                for h in range(HALVES):
                    dve.wait_ge(z_mm[h], i + 1)
                    dve.wait_ge(r_const[h], i + 1)
                    if not (isinstance(i, int) and i == 0):
                        dve.wait_ge(stored[h], 16 * i)
                    V.scalar_tensor_tensor(o_half[h][:, :], ps_z[h][:, :], row(out_scale, h), r_half[h][:, :],
                                           ALU.mult, ALU.add).then_inc(o_ready[h], 1)

            octet(0)
            with dve.Fori(1, NOCT - 2) as i:
                octet(i)
            octet(NOCT - 2, start=False)
            octet(NOCT - 1, walk=False, start=False)

        @block.tensor
        def _(pe):
            mm = nc.tensor.matmul

            pe.wait_ge(ld_style, 16)
            for l in range(LAYERS):
                last = mm(ps_z[0][:, l * B:(l + 1) * B], style_sb[:, l * P:(l + 1) * P],
                          style_sb[:, LAYERS * P:], start=True, stop=True)
            last.then_inc(sty_mm, 1)
            pe.wait_ge(sty2_ready, 1)
            for l in range(LAYERS):
                last = mm(ps_z[1][:, l * B:(l + 1) * B], wsum2r[:, l, :, :].rearrange("i r o -> i (r o)"),
                          sty2[0:C, l, :], start=True, stop=True)
            last.then_inc(dem_mm, 1)

            def walk_t_to_v():
                va, vb = ps_av[:, 0:OCT * C], ps_av[:, OCT * C:]
                mm(va, window(s2t, 0), a_t[:, 1, :, :].rearrange("p b c -> p (b c)"), start=True, stop=True)
                mm(vb, window(s2t, 2), a_t[:, 0, :, :].rearrange("p b c -> p (b c)"),
                   start=True, stop=True).then_inc(av_mm, 1)

            def walk_v_to_y0():
                a, b = (a_v[:, s, :, :].rearrange("p b c -> p (b c)") for s in range(2))
                lo, hi = ps_ay0[:, 0:OCT * C], ps_ay0[:, OCT * C:]
                mm(lo, window(s1t, 2), a, start=True, stop=False)
                mm(lo, window(s1t, 0), b, start=False, stop=True)
                mm(hi, window(s1t, 6), a, start=True, stop=False)
                mm(hi, window(s1t, 4), b, start=False, stop=True).then_inc(ay0_mm, 1)

            def walk_y0_to_x():
                a, b = (a_y0[:, s, :, :].rearrange("p b c -> p (b c)") for s in range(2))
                lo, hi = ps_h[:, 0:OCT * C], ps_h[:, OCT * C:]
                mm(ps_h4[0:C, 0:OCT * C], window(s0t, 4, 1), b, start=True, stop=True)
                mm(lo, window(s0t, 0), a, start=True, stop=True)
                mm(hi, window(s0t, 4), a, start=True, stop=False)
                mm(hi, window(s0t, 0), b, start=False, stop=True).then_inc(h_mm, 1)

            def ends(groups, sem_inc):
                for terms in groups:
                    for k, (dst, w, m) in enumerate(terms):
                        last = mm(dst, w, m, start=(k == 0), stop=(k == len(terms) - 1))
                last.then_inc(sem_inc, 1)

            pe.wait_ge(strip_t, POS)
            pe.wait_ge(at_ready, 1)
            walk_t_to_v()
            pe.wait_ge(strip_f, POS)
            pe.wait_ge(e_in, 1)
            p0 = ps_y[0]
            ends([[(p0[:, 0:B], window(s0f, 4), e_x[:, 2, :]), (p0[:, 0:B], window(s0f, 0), e_x[:, 3, :])],
                  [(p0[:, B:2 * B], window(s0f, 4), e_x[:, 3, :]), (p0[:, B:2 * B], window(s0f, 8), e_x[:, 2, :])],
                  [(p0[:, 2 * B:3 * B], window(s0f, 4), e_x[:, 0, :]),
                   (p0[:, 2 * B:3 * B], window(s0f, 0), e_x[:, 1, :])],
                  [(p0[:, 3 * B:4 * B], window(s0f, 4), e_x[:, 1, :]),
                   (p0[:, 3 * B:4 * B], window(s0f, 8), e_x[:, 0, :])]], edge_mm)
            pe.wait_ge(av_ready, 1)
            walk_v_to_y0()
            pe.wait_ge(e_stage, 1)
            p1 = ps_y[1]
            v0, v1, v2l, vmr = 0, 3 * B, 6 * B, 7 * B
            ends([[(p1[:, v0:v0 + 3 * B], window(s1f, 4), e_y0[:, 1, ALL]),
                   (p1[:, v0 + B:v0 + 3 * B], window(s1f, 12), e_y0[:, 0, CONST_RIGHT])],
                  [(p1[:, v1:v1 + 3 * B], window(s1f, 8), e_y0[:, 1, ALL]),
                   (p1[:, v1:v1 + 2 * B], window(s1f, 0), e_y0[:, 2, LEFT_CONST])],
                  [(p1[:, v2l:v2l + B], window(s1f, 4), e_y0[:, 2, LEFT]),
                   (p1[:, v2l:v2l + B], window(s1f, 12), e_y0[:, 1, LEFT])],
                  [(p1[:, vmr:vmr + B], window(s1f, 8), e_y0[:, 0, RIGHT]),
                   (p1[:, vmr:vmr + B], window(s1f, 0), e_y0[:, 1, RIGHT])]], edge_mm)
            pe.wait_ge(ay0_ready, 1)
            pe.wait_ge(strip_t, 2 * POS)
            walk_y0_to_x()
            pe.wait_ge(lora_ready, 1)
            pe.wait_ge(ld_lora_a, 16)
            for q in range(POS):
                if q >= 2:
                    pe.wait_ge(lora_added, q - 1)
                mm((ps_z[1], ps_ay0)[q % 2][:, :], lora_a_sb[:, :, q], lora_bc[:, :],
                   start=True, stop=True).then_inc(lora_mm, 1)
                if q == 1:
                    pe.wait_ge(e_stage, 2)
                    pe.wait_ge(strip_f, 2 * POS)
                    p2 = ps_z[0]
                    ev = e_v
                    V0, V1 = slice(0, 3 * B), slice(3 * B, 6 * B)
                    v0l, v0c, v0r = (slice(k * B, (k + 1) * B) for k in (0, 1, 2))
                    v1l, v1c, v1r = (slice(k * B, (k + 1) * B) for k in (3, 4, 5))
                    V2L, VMR = slice(6 * B, 7 * B), slice(7 * B, 8 * B)
                    ends([[(p2[:, V0], window(s2f, 4), ev[:, V0]), (p2[:, V0], window(s2f, 0), ev[:, V1]),
                           (p2[:, v0r], window(s2f, 8), ev[:, VMR]), (p2[:, v0c], window(s2f, 8), ev[:, v1c])],
                          [(p2[:, V1], window(s2f, 4), ev[:, V1]), (p2[:, V1], window(s2f, 8), ev[:, V0]),
                           (p2[:, v1l], window(s2f, 0), ev[:, V2L]), (p2[:, v1c], window(s2f, 0), ev[:, v0c])],
                          [(p2[:, V2L], window(s2f, 4), ev[:, V2L]), (p2[:, V2L], window(s2f, 8), ev[:, v1l])],
                          [(p2[:, VMR], window(s2f, 4), ev[:, VMR]), (p2[:, VMR], window(s2f, 0), ev[:, v0r])]],
                         edge_mm)
            pe.wait_ge(e_stage, 3)
            pe.wait_ge(h_ready, 1)
            t0l, t0c, t0r, t1l, t1c, t1r, t2l, tmr = (e_t[:, k * B:(k + 1) * B] for k in range(8))
            w = [window(s3f, 6 - 2 * m) for m in range(4)]
            yl, yr, yc = (ps_h4[0:B, k * P:(k + 1) * P] for k in range(3))
            yk = ps_h4[:, 3 * P:3 * P + B]
            ends([[(yl, t0l, w[1]), (yl, t1l, w[2]), (yl, t2l, w[3])],
                  [(yr, tmr, w[0]), (yr, t0r, w[1]), (yr, t1r, w[2])],
                  [(yc, t1c, w[0]), (yc, t0c, w[1]), (yc, t1c, w[2]), (yc, t0c, w[3])],
                  [(yk, w[0], t1c), (yk, w[1], t0c), (yk, w[2], t1c), (yk, w[3], t0c)]], edge_mm)
            pe.wait_ge(wfold_ready, 1)
            mm(ps_ay0[:, :], ones[:, :], w_fold[:, :], start=True, stop=True).then_inc(wtot_mm, 1)

            def convolve(h):
                for b in range(QUAD):
                    s = h * QUAD + b
                    for g in range(3):
                        last = mm(ps_y[h][:, b * P:(b + 1) * P], x_half[h][:, b, g:g + J],
                                  taps[:, g, :, s, :], start=(g == 0), stop=(g == 2))
                last.then_inc(conv_mm[h], 1)

            def feed_forward(h):
                for q in range(POS):
                    last = mm(ps_z[h][:, :], y_half[h][:, q, :, :].rearrange("j b c -> j (b c)"), w_eff[:, q, :],
                              start=(q == 0), stop=(q == POS - 1))
                last.then_inc(z_mm[h], 1)

            def octet(i, last_octet):
                if not last_octet:
                    pe.wait_ge(at_ready, i + 2)
                    walk_t_to_v()
                pe.wait_ge(ld_x[0], 16 * (i + 1))
                pe.wait_ge(taps_in, 48 * (i + 1))
                pe.wait_ge(taps_in2, 48 * (i + 1))
                convolve(0)
                if not last_octet:
                    pe.wait_ge(av_ready, i + 2)
                    if isinstance(i, int):
                        pe.wait_ge(wtot_copied, 1)
                    walk_v_to_y0()
                pe.wait_ge(ld_x[1], 16 * (i + 1))
                convolve(1)
                if not last_octet:
                    pe.wait_ge(ay0_ready, i + 2)
                    walk_y0_to_x()
                for h in range(HALVES):
                    pe.wait_ge(ends_in[h], 16 * (i + 1))
                    if not (isinstance(i, int) and i == 0):
                        pe.wait_ge(o_ready[h], i)
                    feed_forward(h)

            octet(0, False)
            with pe.Fori(1, NOCT - 1) as i:
                octet(i, False)
            octet(NOCT - 1, True)


_OUT = (B, C, L)


def kernel(**inputs):
    import concourse.bacc as bacc
    from concourse.bass_utils import run_bass_kernel_spmd

    a = {k: np.asarray(v) for k, v in inputs.items()}
    w = a["L0_cond_weights"]
    rev = w[:, :, :, ::-1]
    kinds = [w[0].transpose(0, 2, 1), rev[0].transpose(1, 2, 0),
             w[1].transpose(0, 2, 1), rev[1].transpose(1, 2, 0),
             w[2].transpose(0, 2, 1), rev[2].transpose(1, 2, 0),
             rev[3].transpose(1, 2, 0)]
    wpack = np.tile(np.stack(kinds, 1).reshape(C, 7 * K * C), (POS, 1))
    mod = a["L0_cond_mod_w"].transpose(2, 0, 1)
    mod = np.broadcast_to(mod[:, :, None, :], (STYLE, LAYERS, POS, C)).reshape(STYLE, LAYERS * P)
    style = np.concatenate([mod, a["cond_512"].T], 1)
    lw = np.broadcast_to(a["L0_ffn_lora_weights"][:, None], (8, 16)).reshape(P, 1)
    cols = np.concatenate([np.tile(a["L0_cond_mod_b"].T, (POS, 1)), np.tile(a["L0_cond_biases"].T, (POS, 1)), lw], 1)
    x = a["x"]
    blocks = x.reshape(B, C, J, POS).transpose(3, 1, 0, 2).reshape(P, B, J)
    arrays = {
        "wpack": wpack, "style": style, "cols": cols,
        "lora_a": a["L0_ffn_lora_A"].reshape(RANKS, L),
        "lora_b": a["L0_ffn_lora_B"].transpose(0, 2, 1).reshape(RANKS, L),
        "wt": a["L0_ffn_W"].T.reshape(P, POS * L),
        "bias": a["L0_ffn_bias"].reshape(1, L),
        "x_blocks": blocks,
        "x_edges": blocks[:, :, [0, 1, J - 2, J - 1]].transpose(0, 2, 1),
        "x_rows": x.reshape(B * C, L),
    }
    arrays = {k: np.ascontiguousarray(v) for k, v in arrays.items()}
    nc = bacc.Bacc("TRN2", target_bir_lowering=False, num_devices=1)
    args = [nc.dram_tensor(k, v.shape, F32, kind="ExternalInput").ap() for k, v in arrays.items()]
    res = nc.dram_tensor("out", (B * C, L), F32, kind="ExternalOutput").ap()
    build(nc, *args, res)
    r = run_bass_kernel_spmd(nc, [arrays], core_ids=[0])
    return r.results[0]["out"].reshape(_OUT)
```

```python
from contextlib import ExitStack

import numpy as np

import concourse.bass as bass
from concourse import mybir

F32 = mybir.dt.float32
F32R = mybir.dt.float32r
ALU = mybir.AluOpType
ACT = mybir.ActivationFunctionType

B, C, L = 64, 32, 512
LAYERS, K, STYLE = 4, 3, 64
RANKS = 128
P = 128
POS = P // C
J = L // POS
OCT = 8
QUAD = 4
NOCT = B // OCT
HALVES = OCT // QUAD
TAPS = 6
SCALE = 1.0 / float(np.sqrt(C * K ** 2))
LORA_SCALE = 32 / 16
EPS = 1e-8
SPLIT = [(1, 0), (0, 1), (0, 0)]
BLUR = [1 / 8, 3 / 8, 3 / 8, 1 / 8]
W0T, W2T, W1F, W0F, W1T, W2F, W3F = range(7)


def build(nc, wpack, style, cols, lora_a, lora_b, wt, bias, x_blocks, x_edges, x_rows, out):
    ctx = ExitStack()
    with ctx:
        def sb(name, shape, dtype=F32):
            return ctx.enter_context(nc.sbuf_tensor(name, shape, dtype))

        def pair(name, shape):
            return [sb(f"{name}_hi", shape, F32R), sb(f"{name}_lo", shape, F32R)]

        def pb(name, shape):
            return ctx.enter_context(nc.psum_tensor(name, shape, F32))

        def sem(name):
            return ctx.enter_context(nc.semaphore(name))

        w_sb = sb("w_sb", [P, 7, K * C])
        style_sb = sb("style_sb", [STYLE, LAYERS * P + B])
        cols_sb = sb("cols_sb", [P, 9])
        lora_a_sb = sb("lora_a_sb", [P, J, POS])
        lora_b_sb = sb("lora_b_sb", [P, L])
        w_eff = sb("w_eff", [P, POS, L])
        bias_sb = sb("bias_sb", [P, L])
        x_edge = sb("x_edge", [P, 4, B])
        x_half = [sb(f"x_half{h}", [P, QUAD, J + 2]) for h in range(HALVES)]
        blur1 = sb("blur1", [P, TAPS * C])
        blur1r = sb("blur1r", [P, TAPS * C])
        blur3r = sb("blur3r", [P, TAPS * C])
        s0t = sb("s0t", [P, 8 * C])
        s2t = sb("s2t", [P, 6 * C])
        s1t = sb("s1t", [P, 10 * C])
        s0f = sb("s0f", [P, 12 * C])
        s2f = sb("s2f", [P, 12 * C])
        s1f = sb("s1f", [P, 16 * C])
        s3f = sb("s3f", [P, 10 * C])
        w3_taps = sb("w3_taps", [P, 2, C])
        sty = sb("sty", [P, LAYERS, B])
        sty2 = sb("sty2", [P, LAYERS, B])
        root = sb("root", [P, LAYERS, B])
        root01 = sb("root01", [P, B])
        dem1 = sb("dem1", [P, B])
        dem2 = sb("dem2", [P, B])
        dem3 = sb("dem3", [P, B])
        eps_col = sb("eps_col", [P, 1])
        act_warm = sb("act_warm", [P, 1])
        wsq = sb("wsq", [C, LAYERS, K, C])
        wsum2 = sb("wsum2", [C, LAYERS, C])
        wsum2r = sb("wsum2r", [C, LAYERS, POS, C])
        sc_t = sb("sc_t", [P, B])
        sc_v = sb("sc_v", [P, B])
        sc_y0 = sb("sc_y0", [P, B])
        bs_y0 = sb("bs_y0", [P, B])
        bs_v = sb("bs_v", [P, B])
        bs_t = sb("bs_t", [P, B])
        bs_end = sb("bs_end", [P, B])
        out_scale = sb("out_scale", [P, B // QUAD])
        out_const = sb("out_const", [P, B // QUAD])
        const_rep = sb("const_rep", [P, B])
        a_t = sb("a_t", [P, 2, OCT, C])
        a_v = sb("a_v", [P, 2, OCT, C])
        a_y0 = sb("a_y0", [P, 2, OCT, C])
        taps = sb("taps", [P, 3, POS, OCT, C])
        e_x = sb("e_x", [P, 4, B])
        e_y0 = sb("e_y0", [P, 7, B])
        e_v = sb("e_v", [P, 8, B])
        e_t = sb("e_t", [P, 8, B])
        e_const = sb("e_const", [P, B])
        e_diff = sb("e_diff", [P, 2, B])
        e_out = pair("e_out", [P, P])
        ident = sb("ident", [P, P])
        y_half = [pair(f"y_half{h}", [P, POS, QUAD, C]) for h in range(HALVES)]
        w_pair = pair("w_pair", [P, POS, L])
        r_half = [sb(f"r_half{h}", [P, L]) for h in range(HALVES)]
        o_half = [sb(f"o_half{h}", [P, L]) for h in range(HALVES)]
        coef = sb("coef", [P, 1])
        lora_bc = sb("lora_bc", [P, L])
        w_part = sb("w_part", [P, 2, L])
        w_fold = sb("w_fold", [P, L])
        w_total = sb("w_total", [P, L])
        ones = sb("ones", [P, P])

        ps_y = [pb(f"ps_y{h}", [P, L]) for h in range(HALVES)]
        ps_z = [pb(f"ps_z{h}", [P, L]) for h in range(HALVES)]
        ps_av = pb("ps_av", [P, L])
        ps_ay0 = pb("ps_ay0", [P, L])
        ps_h = pb("ps_h", [P, L])
        ps_h4 = pb("ps_h4", [P, L])

        LORA_BANK = [ps_ay0, ps_h, ps_h4, ps_y[1]]

        e_dram = nc.dram_tensor("edge_rows", [2, 2, POS, B, C], F32, kind="Internal").ap()

        ld_style = sem("ld_style")
        ld_cols = sem("ld_cols")
        ld_w = sem("ld_w")
        ld_xe = sem("ld_xe")
        ld_wt = sem("ld_wt")
        ld_lora_a = sem("ld_lora_a")
        ld_lora_b = sem("ld_lora_b")
        ld_bias = sem("ld_bias")
        ld_x = [sem(f"ld_x{h}") for h in range(HALVES)]
        ld_r = [sem(f"ld_r{h}") for h in range(HALVES)]
        zeroed = sem("zeroed")
        taps_zeroed = sem("taps_zeroed")
        ident_zero = sem("ident_zero")
        ident_ready = sem("ident_ready")
        strip_t = sem("strip_t")
        strip_s1t = sem("strip_s1t")
        strip_f = sem("strip_f")
        ve = sem("ve")
        coef_ready = sem("coef_ready")
        sty_ready = sem("sty_ready")
        demod_in = sem("demod_in")
        blur3_ready = sem("blur3_ready")
        blur1_ready = sem("blur1_ready")
        sty_mm = sem("sty_mm")
        dem_mm = sem("dem_mm")
        rooted = sem("rooted")
        lora_mm = sem("lora_mm")
        lora_added = sem("lora_added")
        w_high = sem("w_high")
        w_low = sem("w_low")
        w_parts = sem("w_parts")
        wfold_ready = sem("wfold_ready")
        wtot_mm = sem("wtot_mm")
        wtot_copied = sem("wtot_copied")
        e_in = sem("e_in")
        edge_mm = sem("edge_mm")
        e_stage = sem("e_stage")
        turned_mm = sem("turned_mm")
        lora_ready = sem("lora_ready")
        e_rows = sem("e_rows")
        edge_written = sem("edge_written")
        at_ready = sem("at_ready")
        av_mm = sem("av_mm")
        av_ready = sem("av_ready")
        ay0_mm = sem("ay0_mm")
        ay0_ready = sem("ay0_ready")
        h_mm = sem("h_mm")
        h_ready = sem("h_ready")
        taps_in = sem("taps_in")
        taps_moved = sem("taps_moved")
        conv_mm = [sem(f"conv_mm{h}") for h in range(HALVES)]
        y_high = [sem(f"y_high{h}") for h in range(HALVES)]
        y_low = [sem(f"y_low{h}") for h in range(HALVES)]
        ends_in = [sem(f"ends_in{h}") for h in range(HALVES)]
        z_mm = [sem(f"z_mm{h}") for h in range(HALVES)]
        r_biased = [sem(f"r_biased{h}") for h in range(HALVES)]
        r_const = [sem(f"r_const{h}") for h in range(HALVES)]
        o_ready = [sem(f"o_ready{h}") for h in range(HALVES)]
        stored = [sem(f"stored{h}") for h in range(HALVES)]

        block = ctx.enter_context(nc.Block())

        def window(strip, first, n=POS):
            return strip[:, first * C:(first + n) * C]

        def over_c(t, n=C):
            return t.unsqueeze(2).broadcast_to([P, OCT, n])

        def every_other(t, q, k0):
            return t[q, :].rearrange("c (k o) -> c k o", o=C)[:, k0:min(k0 + 5, TAPS):2, :]

        @block.sync
        def _(sp):
            sp.dma_start(style_sb[:, :], style).then_inc(ld_style, 16)
            sp.dma_start(w_sb[:, :, :].rearrange("p k f -> p (k f)"), wpack).then_inc(ld_w, 16)
            sp.dma_start(x_edge[:, :, :], x_edges).then_inc(ld_xe, 16)
            sp.dma_start(w_eff[:, :, :].rearrange("p q o -> p (q o)"), wt).then_inc(ld_wt, 16)
            sp.wait_ge(zeroed, 1)
            for h in range(HALVES):
                sp.dma_start(x_half[h][:, :, 1:1 + J], x_blocks[:, h * QUAD:(h + 1) * QUAD, :]).then_inc(ld_x[h], 16)
            for h in range(HALVES):
                sp.dma_start(r_half[h][:, :], x_rows[h * P:(h + 1) * P, :]).then_inc(ld_r[h], 16)

            def shift_taps(n):
                sp.wait_ge(h_ready, n + 1)
                sp.dma_start(taps[C:P, :, 1, :, :], taps[0:P - C, :, 0, :, :]).then_inc(taps_in, 16)
                sp.dma_start(taps[0:3 * C, 1:3, 3, :, :], taps[C:P, 0:2, 0, :, :]).then_inc(taps_in, 16)

            shift_taps(0)
            sp.wait_ge(e_rows, 1)
            for part in range(2):
                for side in range(2):
                    sp.dma_start(e_dram[part, side].rearrange("q b c -> b q c"),
                                 e_out[part][side * B:(side + 1) * B, :].bitcast(F32)
                                 .rearrange("b (q c) -> b q c", q=POS)).then_inc(edge_written, 16)

            def octet(i, last):
                if not last:
                    for h in range(HALVES):
                        sp.wait_ge(conv_mm[h], i + 1)
                        sp.dma_start(x_half[h][:, :, 1:1 + J],
                                     x_blocks[:, bass.ds((i + 1) * OCT + h * QUAD, QUAD), :]).then_inc(ld_x[h], 16)
                    shift_taps(i + 1)
                for h in range(HALVES):
                    sp.wait_ge(o_ready[h], i + 1)
                    sp.dma_start(out[bass.ds((i * HALVES + h) * P, P), :], o_half[h][:, :]).then_inc(stored[h], 16)
                    if not last:
                        sp.dma_start(r_half[h][:, :],
                                     x_rows[bass.ds(((i + 1) * HALVES + h) * P, P), :]).then_inc(ld_r[h], 16)

            with sp.Fori(0, NOCT - 1) as i:
                octet(i, False)
            octet(NOCT - 1, True)
            for h in range(HALVES):
                sp.wait_ge(stored[h], 16 * NOCT)

        @block.gpsimd
        def _(pool):
            nc.gpsimd.memset(eps_col[:, :], EPS)
            for t in (blur3r, blur1r, blur1, s2t, s0t, s0f, s1t, s2f, s3f, s1f):
                nc.gpsimd.memset(t[:, :], 0.0)
            for h in range(HALVES):
                nc.gpsimd.memset(x_half[h][:, :, 0:J + 2:J + 1], 0.0)
            nc.gpsimd.memset(ones[:, :], 1.0).then_inc(zeroed, 1)
            pool.wait_ge(zeroed, 1)
            pool.wait_ge(ld_w, 16)
            for strip, kind in ((s2t, W2T), (s0t, W0T)):
                for p in range(POS):
                    q = slice(p * C, (p + 1) * C)
                    nc.gpsimd.tensor_copy(strip[q, p * C:(p + K) * C], w_sb[q, kind, :]).then_inc(strip_t, 1)
            pool.wait_ge(strip_t, 2 * POS)
            pool.wait_ge(ld_xe, 16)
            pool.wait_ge(sty_ready, 1)
            nc.gpsimd.tensor_tensor(e_x[:, :, :], x_edge[:, :, :], sty[:, 0:1, :].broadcast_to([P, 4, B]),
                                    ALU.mult).then_inc(e_in, 1)
            pool.wait_ge(e_in, 1)
            nc.gpsimd.memset(taps[:, 2, 0, :, :], 0.0)
            nc.gpsimd.memset(taps[:, 0, :, :, :], 0.0).then_inc(taps_zeroed, 1)
            nc.gpsimd.memset(ident[:, :], 0.0).then_inc(ident_zero, 1)
            pool.wait_ge(ident_zero, 1)
            nc.gpsimd.affine_select(out=ident[:, :], in_=ident[:, :], compare_op=ALU.not_equal, fill=1.0, base=0,
                                    pattern=[[-1, P]], channel_multiplier=1).then_inc(ident_ready, 1)
            pool.wait_ge(ident_ready, 1)
            for q in range(POS):
                pool.wait_ge(w_high, q + 1)
                nc.gpsimd.tensor_tensor(w_pair[1][:, q, :], w_eff[:, q, :], w_pair[0][:, q, :].bitcast(F32),
                                        ALU.subtract).then_inc(w_low, 1)
                pool.wait_ge(w_low, q + 1)
            pool.wait_ge(lora_added, POS)
            for k in range(2):
                nc.gpsimd.tensor_tensor(w_part[:, k, :], w_eff[:, 2 * k, :], w_eff[:, 2 * k + 1, :],
                                        ALU.add).then_inc(w_parts, 1)
                pool.wait_ge(w_parts, k + 1)
            nc.gpsimd.tensor_tensor(w_fold[:, :], w_part[:, 0, :], w_part[:, 1, :], ALU.add).then_inc(wfold_ready, 1)
            pool.wait_ge(wfold_ready, 1)
            pool.wait_ge(ld_bias, 16)

            def octet(i):
                for h in range(HALVES):
                    pool.wait_ge(ld_r[h], 16 * (i + 1))
                    nc.gpsimd.tensor_tensor(r_half[h][:, :], r_half[h][:, :], bias_sb[:, :],
                                            ALU.add).then_inc(r_biased[h], 1)
                    pool.wait_ge(r_biased[h], i + 1)

            with pool.Fori(0, NOCT) as i:
                octet(i)

        @block.scalar
        def _(act):
            act.dma_start(cols_sb[:, :], cols).then_inc(ld_cols, 16)
            act.dma_start(lora_b_sb[:, :], lora_b).then_inc(ld_lora_b, 16)
            act.dma_start(lora_a_sb[:, :, :].rearrange("r j q -> r (j q)"), lora_a).then_inc(ld_lora_a, 16)
            act.dma_start(bias_sb[:, :], bias.broadcast_to([P, L])).then_inc(ld_bias, 16)
            act.wait_ge(zeroed, 1)
            nc.scalar.activation(act_warm[:, :], eps_col[:, :], ACT.Sqrt)
            act.wait_ge(ld_cols, 16)
            nc.scalar.mul(coef[:, :], cols_sb[:, 8:9], LORA_SCALE).then_inc(coef_ready, 1)
            act.wait_ge(coef_ready, 1)
            act.wait_ge(ld_lora_b, 16)
            nc.scalar.activation(lora_bc[:, :], lora_b_sb[:, :], ACT.Copy, scale=coef[:, 0:1]).then_inc(lora_ready, 1)

            def place(strip, at, src, n):
                for p in range(POS):
                    q = slice(p * C, (p + 1) * C)
                    nc.scalar.activation(strip[q, at(p) * C:(at(p) + n) * C].rearrange("c (k o) -> c k o", o=C),
                                         src(p, q), ACT.Copy).then_inc(strip_f, 1)

            act.wait_ge(ld_w, 16)
            place(s0f, lambda p: p + 3, lambda p, q: w_sb[q, W0F, :].rearrange("c (k o) -> c k o", o=C), K)
            act.wait_ge(dem_mm, 1)
            nc.scalar.activation(root[:, :, :].rearrange("p l b -> p (l b)"), ps_z[1][:, 0:LAYERS * B],
                                 ACT.Sqrt, bias=eps_col[:, :]).then_inc(rooted, 1)
            place(s2f, lambda p: p + 3, lambda p, q: w_sb[q, W2F, :].rearrange("c (k o) -> c k o", o=C), K)
            act.wait_ge(blur3_ready, 1)
            place(s3f, lambda p: p // 2 + 3, lambda p, q: every_other(blur3r, q, 3 - p + 2 * (p // 2 - 1)), 3)
            act.wait_ge(blur1_ready, 1)
            place(s1f, lambda p: 2 * p + 2, lambda p, q: blur1[q, :].rearrange("c (k o) -> c k o", o=C), TAPS)

            for q in range(POS):
                act.wait_ge(lora_added, q + 1)
                nc.scalar.activation(w_pair[0][:, q, :], w_eff[:, q, :], ACT.Copy).then_inc(w_high, 1)

            def shift_taps(n):
                act.wait_ge(h_ready, n + 1)
                for q, rows, src, blocks in ((2, slice(64, P), slice(0, 64), slice(0, 3)),
                                             (2, slice(0, 64), slice(64, P), slice(1, 3)),
                                             (3, slice(96, P), slice(0, 32), slice(0, 3)),
                                             (1, slice(0, 32), slice(96, P), slice(1, 3))):
                    before = slice(blocks.start - 1, blocks.stop - 1) if blocks.start else blocks
                    nc.scalar.activation(taps[rows, blocks, q, :, :].rearrange("p g b c -> p g (b c)"),
                                         taps[src, before, 0, :, :].rearrange("p g b c -> p g (b c)"),
                                         ACT.Copy).then_inc(taps_moved, 1)

            def octet(i, shift=True):
                for h in range(HALVES):
                    act.wait_ge(conv_mm[h], i + 1)
                    if not (isinstance(i, int) and i == 0):
                        act.wait_ge(z_mm[h], i)
                    nc.scalar.activation(y_half[h][0][:, :, :, :].rearrange("j q b c -> j b q c"),
                                         ps_y[h][:, :].rearrange("j (b q c) -> j b q c", b=QUAD, q=POS),
                                         ACT.Copy).then_inc(y_high[h], 1)
                    if isinstance(i, int) and i == 0:
                        act.wait_ge(edge_written, 64)
                    act.wait_ge(y_low[h], i + 1)
                    for part in range(2):
                        act.dma_start(y_half[h][part][0:P:P - 1, :, :, :].bitcast(F32),
                                      e_dram[part, :, :, bass.ds(i * OCT + h * QUAD, QUAD), :]
                                      ).then_inc(ends_in[h], 16)

                if shift:
                    shift_taps(i + 1)

            shift_taps(0)
            octet(0)
            with act.Fori(1, NOCT - 1) as i:
                octet(i)
            octet(NOCT - 1, shift=False)

        @block.vector
        def _(dve):
            done = [0]

            def link(ins):
                done[0] += 1
                ins.then_inc(ve, 1)
                dve.wait_ge(ve, done[0])

            V = nc.vector
            dve.wait_ge(sty_mm, 1)
            dve.wait_ge(ld_cols, 16)
            for l in range(LAYERS):
                last = V.tensor_scalar(sty[:, l, :], ps_z[0][:, l * B:(l + 1) * B], cols_sb[:, l:l + 1], SCALE,
                                       ALU.add, ALU.mult)
            last.then_inc(sty_ready, 1)
            dve.wait_ge(ld_w, 16)
            flat = wsq[:, :, :, :].rearrange("p l k c -> p (l k c)")
            w4 = w_sb[0:C, W0F:W3F + 1, :].rearrange("p l f -> p (l f)")
            link(V.tensor_tensor(flat, w4, w4, ALU.mult))
            V.tensor_tensor(sty2[:, :, :], sty[:, :, :], sty[:, :, :], ALU.mult)
            link(V.tensor_tensor(wsum2[:, :, :], wsq[:, :, 0, :], wsq[:, :, 1, :], ALU.add))
            V.tensor_tensor(wsum2r[:, :, :, :], wsum2[:, :, :].unsqueeze(2).broadcast_to([C, LAYERS, POS, C]),
                            wsq[:, :, 2, :].unsqueeze(2).broadcast_to([C, LAYERS, POS, C]),
                            ALU.add).then_inc(demod_in, 1)

            def blur(j, *kernels, signal=None):
                for dst, kind, gain in kernels:
                    part = dst[:, j * C:(j + K) * C]
                    last = V.scalar_tensor_tensor(part, w_sb[:, kind, :], gain * BLUR[j], part, ALU.mult, ALU.add)
                if signal is None:
                    link(last)
                else:
                    last.then_inc(signal, 1)

            dve.wait_ge(zeroed, 1)
            blur(0, (blur3r, W3F, 1.0))
            V.tensor_scalar(bs_end[:, :], sty[:, 2, :], cols_sb[:, 5:6], -2.0 * BLUR[0], ALU.mult, ALU.mult)
            blur(1, (blur3r, W3F, 1.0))
            V.tensor_scalar(bs_v[:, :], sty[:, 2, :], cols_sb[:, 5:6], 2.0, ALU.mult, ALU.mult)
            blur(2, (blur3r, W3F, 1.0))
            V.tensor_scalar(bs_t[:, :], sty[:, 3, :], cols_sb[:, 6:7], None, ALU.mult)
            blur(3, (blur3r, W3F, 1.0))
            V.tensor_tensor(sc_v[:, :], sty[:, 2, :], sty[:, 1, :], ALU.mult)
            for p in range(POS):
                q = slice(p * C, (p + 1) * C)
                src = blur3r[q, :].rearrange("c (k o) -> c k o", o=C)[:, 3 - p:6 - p:2, :]
                last = V.tensor_copy(w3_taps[q, :, :], src)
            last.then_inc(blur3_ready, 1)
            for j in (0, 1):
                blur(j, (blur1r, W1T, 2.0), (blur1, W1F, 2.0))
            dve.wait_ge(rooted, 1)
            link(V.reciprocal(dem2[:, :], root[:, 2, :]))
            link(V.tensor_tensor(sc_t[:, :], sty[:, 3, :], dem2[:, :], ALU.mult))

            def start_taps(col):
                for slot in range(2):
                    last = V.tensor_tensor(a_t[:, slot, :, :],
                                           w3_taps[:, slot, :].unsqueeze(1).broadcast_to([P, OCT, C]),
                                           over_c(sc_t[:, col]), ALU.mult)
                last.then_inc(at_ready, 1)

            start_taps(slice(0, OCT))
            V.tensor_tensor(root01[:, :], root[:, 0, :], root[:, 1, :], ALU.mult)
            blur(2, (blur1r, W1T, 2.0), (blur1, W1F, 2.0))
            blur(3, (blur1r, W1T, 2.0), (blur1, W1F, 2.0), signal=blur1_ready)
            dve.wait_ge(blur1_ready, 1)
            for p in range(POS):
                q = slice(p * C, (p + 1) * C)
                first = {0: -2, 1: -1, 2: -1, 3: 0}[p]
                last = V.tensor_copy(s1t[q, (first + 4) * C:(first + 7) * C].rearrange("c (k o) -> c k o", o=C),
                                     every_other(blur1r, q, 4 - p + 2 * first))
            last.then_inc(strip_s1t, 1)

            def scale_av(col):
                V.tensor_tensor(a_v[:, :, :, :], ps_av[:, :].rearrange("p (s b c) -> p s b c", s=2, b=OCT),
                                sc_v[:, col].unsqueeze(1).unsqueeze(3).broadcast_to([P, 2, OCT, C]),
                                ALU.mult).then_inc(av_ready, 1)

            def scale_ay0(col):
                V.tensor_tensor(a_y0[:, :, :, :], ps_ay0[:, :].rearrange("p (s b c) -> p s b c", s=2, b=OCT),
                                sc_y0[:, col].unsqueeze(1).unsqueeze(3).broadcast_to([P, 2, OCT, C]),
                                ALU.mult).then_inc(ay0_ready, 1)

            def scale_h(col):
                V.tensor_tensor(taps[:, 0:2, 0, :, :], ps_h[:, :].rearrange("p (s b c) -> p s b c", s=2, b=OCT),
                                sty[:, 0, col].unsqueeze(1).unsqueeze(3).broadcast_to([P, 2, OCT, C]), ALU.mult)
                V.tensor_tensor(taps[0:C, 2, 0, :, :], ps_h4[0:C, 0:OCT * C].rearrange("p (b c) -> p b c", b=OCT),
                                sty[0:C, 0, col].unsqueeze(2).broadcast_to([C, OCT, C]),
                                ALU.mult).then_inc(h_ready, 1)

            def add_lora(q):
                dve.wait_ge(lora_mm, q + 1)
                dve.wait_ge(ld_wt, 16)
                V.tensor_tensor(w_eff[:, q, :], w_eff[:, q, :], LORA_BANK[q][:, :], ALU.add).then_inc(lora_added, 1)

            dve.wait_ge(av_mm, 1)
            scale_av(slice(0, OCT))
            add_lora(0)
            V.reciprocal(dem1[:, :], root[:, 1, :])
            link(V.reciprocal(sc_y0[:, :], root01[:, :]))
            link(V.tensor_scalar(bs_y0[:, :], dem1[:, :], cols_sb[:, 4:5], None, ALU.mult))
            V.tensor_copy(e_y0[:, 0:7:3, :], bs_y0[:, :].unsqueeze(1).broadcast_to([P, 3, B]))
            dve.wait_ge(edge_mm, 1)
            two = [P, 2, B]
            y0_left, y0_right = e_y0[:, 2:6:3, :], e_y0[:, 1:5:3, :]
            for k, dst in ((0, y0_left), (1, y0_right)):
                last = V.tensor_tensor(dst, ps_y[0][:, 2 * k * B:2 * (k + 1) * B].rearrange("p (k b) -> p k b", b=B),
                                       sc_y0[:, :].unsqueeze(1).broadcast_to(two), ALU.mult)
            link(last)
            for dst in (y0_left, y0_right):
                last = V.tensor_tensor(dst, dst, bs_y0[:, :].unsqueeze(1).broadcast_to(two), ALU.add)
            last.then_inc(e_stage, 1)
            dve.wait_ge(ay0_mm, 1)
            scale_ay0(slice(0, OCT))
            add_lora(1)
            add_lora(2)
            def end_stage(dst, src, scale, shift):
                eight = [P, 8, B]
                link(V.tensor_tensor(dst[:, :, :], src[:, :].rearrange("p (k b) -> p k b", b=B),
                                     scale[:, :].unsqueeze(1).broadcast_to(eight), ALU.mult))
                return V.tensor_tensor(dst[:, :, :], dst[:, :, :], shift[:, :].unsqueeze(1).broadcast_to(eight),
                                       ALU.add)

            dve.wait_ge(edge_mm, 2)
            link(end_stage(e_v, ps_z[0], sc_v, bs_v))
            V.tensor_tensor(e_v[0:C, 0, :], e_v[0:C, 0, :], bs_end[0:C, :], ALU.add)
            V.tensor_tensor(e_v[P - C:P, 7, :], e_v[P - C:P, 7, :], bs_end[P - C:P, :],
                            ALU.add).then_inc(e_stage, 1)
            dve.wait_ge(h_mm, 1)
            dve.wait_ge(taps_zeroed, 1)
            scale_h(slice(0, OCT))
            start_taps(slice(OCT, 2 * OCT))
            add_lora(3)
            V.reciprocal(dem3[:, :], root[:, 3, :])
            dve.wait_ge(edge_mm, 3)
            end_stage(e_t, ps_z[1], sc_t, bs_t).then_inc(e_stage, 1)
            dve.wait_ge(edge_mm, 4)
            link(V.tensor_copy(e_const[:, :], ps_z[0][:, B:2 * B]))
            V.tensor_tensor(e_diff[:, :, :], ps_z[0][:, 0:3 * B].rearrange("p (k b) -> p k b", b=B)[:, 0:3:2, :],
                            e_const[:, :].unsqueeze(1).broadcast_to(two), ALU.subtract).then_inc(e_stage, 1)
            link(V.tensor_tensor(const_rep[:, :], e_const[:, :], dem3[:, :], ALU.mult))
            dve.wait_ge(av_mm, 2)
            scale_av(slice(OCT, 2 * OCT))
            dve.wait_ge(turned_mm, 1)
            link(V.tensor_copy(e_out[0][:, :], ps_z[1][:, 0:P]))
            V.tensor_tensor(e_out[1][:, :], ps_z[1][:, 0:P], e_out[0][:, :].bitcast(F32),
                            ALU.subtract).then_inc(e_rows, 1)
            for r in range(QUAD):
                q = slice(r * C, (r + 1) * C)
                V.tensor_copy(out_scale[q, :], dem3[q, r:B:QUAD])
                last = V.tensor_scalar(out_const[q, :], const_rep[q, r:B:QUAD], cols_sb[q, 7:8], None, ALU.add)
            link(last)

            def copy_w_total():
                dve.wait_ge(wtot_mm, 1)
                V.tensor_copy(w_total[:, :], ps_z[0][:, :]).then_inc(wtot_copied, 1)
                dve.wait_ge(wtot_copied, 1)

            def octet(i, walk=True, start=True):
                def col(n):
                    return slice(n * OCT, (n + 1) * OCT) if isinstance(n, int) else bass.ds(n * OCT, OCT)

                def row(t, h):
                    return t[:, bass.ds(i * HALVES + h, 1)]

                def add_const(h):
                    dve.wait_ge(r_biased[h], i + 1)
                    V.scalar_tensor_tensor(r_half[h][:, :], w_total[:, :], row(out_const, h), r_half[h][:, :],
                                           ALU.mult, ALU.add).then_inc(r_const[h], 1)

                def y_low_part(h):
                    dve.wait_ge(y_high[h], i + 1)
                    V.tensor_tensor(y_half[h][1][:, :, :, :].rearrange("j q b c -> j b q c"),
                                    ps_y[h][:, :].rearrange("j (b q c) -> j b q c", b=QUAD, q=POS),
                                    y_half[h][0][:, :, :, :].bitcast(F32).rearrange("j q b c -> j b q c"),
                                    ALU.subtract).then_inc(y_low[h], 1)

                first = isinstance(i, int) and i == 0
                if walk and not first:
                    dve.wait_ge(av_mm, i + 2)
                    scale_av(col(i + 1))
                y_low_part(0)
                if not first:
                    add_const(0)
                if walk:
                    dve.wait_ge(ay0_mm, i + 2)
                    scale_ay0(col(i + 1))
                y_low_part(1)
                if first:
                    copy_w_total()
                    add_const(0)
                add_const(1)
                if walk:
                    dve.wait_ge(h_mm, i + 2)
                    scale_h(col(i + 1))
                if start:
                    start_taps(col(i + 2))
                for h in range(HALVES):
                    dve.wait_ge(z_mm[h], i + 1)
                    dve.wait_ge(r_const[h], i + 1)
                    if not (isinstance(i, int) and i == 0):
                        dve.wait_ge(stored[h], 16 * i)
                    V.scalar_tensor_tensor(o_half[h][:, :], ps_z[h][:, :], row(out_scale, h), r_half[h][:, :],
                                           ALU.mult, ALU.add).then_inc(o_ready[h], 1)

            octet(0)
            with dve.Fori(1, NOCT - 2) as i:
                octet(i)
            octet(NOCT - 2, start=False)
            octet(NOCT - 1, walk=False, start=False)

        @block.tensor
        def _(pe):
            mm = nc.tensor.matmul

            pe.wait_ge(ld_style, 16)
            for l in range(LAYERS):
                last = mm(ps_z[0][:, l * B:(l + 1) * B], style_sb[:, l * P:(l + 1) * P],
                          style_sb[:, LAYERS * P:], start=True, stop=True)
            last.then_inc(sty_mm, 1)
            pe.wait_ge(lora_ready, 1)
            pe.wait_ge(ld_lora_a, 16)

            def lora(q):
                mm(LORA_BANK[q][:, :], lora_a_sb[:, :, q], lora_bc[:, :],
                   start=True, stop=True).then_inc(lora_mm, 1)

            lora(0)
            pe.wait_ge(demod_in, 1)
            for l in range(LAYERS):
                last = mm(ps_z[1][:, l * B:(l + 1) * B], wsum2r[:, l, :, :].rearrange("i r o -> i (r o)"),
                          sty2[0:C, l, :], start=True, stop=True)
            last.then_inc(dem_mm, 1)
            lora(1)

            def walk_t_to_v():
                va, vb = ps_av[:, 0:OCT * C], ps_av[:, OCT * C:]
                mm(va, window(s2t, 0), a_t[:, 1, :, :].rearrange("p b c -> p (b c)"), start=True, stop=True)
                mm(vb, window(s2t, 2), a_t[:, 0, :, :].rearrange("p b c -> p (b c)"),
                   start=True, stop=True).then_inc(av_mm, 1)

            def walk_v_to_y0():
                a, b = (a_v[:, s, :, :].rearrange("p b c -> p (b c)") for s in range(2))
                lo, hi = ps_ay0[:, 0:OCT * C], ps_ay0[:, OCT * C:]
                mm(lo, window(s1t, 2), a, start=True, stop=False)
                mm(lo, window(s1t, 0), b, start=False, stop=True)
                mm(hi, window(s1t, 6), a, start=True, stop=False)
                mm(hi, window(s1t, 4), b, start=False, stop=True).then_inc(ay0_mm, 1)

            def walk_y0_to_x():
                a, b = (a_y0[:, s, :, :].rearrange("p b c -> p (b c)") for s in range(2))
                lo, hi = ps_h[:, 0:OCT * C], ps_h[:, OCT * C:]
                mm(ps_h4[0:C, 0:OCT * C], window(s0t, 4, 1), b, start=True, stop=True)
                mm(lo, window(s0t, 0), a, start=True, stop=True)
                mm(hi, window(s0t, 4), a, start=True, stop=False)
                mm(hi, window(s0t, 0), b, start=False, stop=True).then_inc(h_mm, 1)

            def accumulate(*terms):
                for k, (dst, w, m) in enumerate(terms):
                    last = mm(dst, w, m, start=(k == 0), stop=(k == len(terms) - 1))
                return last

            def blocks(t, first, n, step=1):
                return t[:, first:first + (n - 1) * step + 1:step, :]

            def banked(ps, first, n, step=1):
                return blocks(ps[:, :].rearrange("p (k b) -> p k b", b=B), first, n, step)

            pe.wait_ge(strip_t, POS)
            pe.wait_ge(at_ready, 1)
            walk_t_to_v()
            pe.wait_ge(strip_f, POS)
            pe.wait_ge(e_in, 1)
            p0 = ps_y[0]
            accumulate((banked(p0, 0, 4), window(s0f, 4), blocks(e_x, 0, 4)),
                       (banked(p0, 0, 2, 2), window(s0f, 0), blocks(e_x, 1, 2, 2)),
                       (banked(p0, 1, 2, 2), window(s0f, 8), blocks(e_x, 0, 2, 2))).then_inc(edge_mm, 1)
            lora(2)
            pe.wait_ge(av_ready, 1)
            pe.wait_ge(strip_s1t, 1)
            pe.wait_ge(lora_added, 1)
            walk_v_to_y0()
            pe.wait_ge(e_stage, 1)
            pe.wait_ge(strip_f, 4 * POS)
            p1 = ps_z[0]
            accumulate((banked(p1, 0, 4), window(s1f, 4), blocks(e_y0, 2, 4)),
                       (banked(p1, 1, 3), window(s1f, 12), blocks(e_y0, 0, 3)))
            accumulate((banked(p1, 4, 4), window(s1f, 8), blocks(e_y0, 1, 4)),
                       (banked(p1, 4, 3), window(s1f, 0), blocks(e_y0, 4, 3))).then_inc(edge_mm, 1)
            lora(3)
            pe.wait_ge(ay0_ready, 1)
            pe.wait_ge(strip_t, 2 * POS)
            pe.wait_ge(lora_added, 3)
            walk_y0_to_x()
            pe.wait_ge(e_stage, 2)
            p2 = ps_z[1]
            accumulate((banked(p2, 0, 8), window(s2f, 4), blocks(e_v, 0, 8)),
                       (banked(p2, 0, 3), window(s2f, 0), blocks(e_v, 5, 3)),
                       (banked(p2, 5, 3), window(s2f, 8), blocks(e_v, 0, 3)),
                       (banked(p2, 4, 2), window(s2f, 0), blocks(e_v, 2, 2)),
                       (banked(p2, 2, 2), window(s2f, 8), blocks(e_v, 4, 2)),
                       (banked(p2, 6, 1), window(s2f, 0), blocks(e_v, 1, 1)),
                       (banked(p2, 1, 1), window(s2f, 8), blocks(e_v, 6, 1)),
                       ).then_inc(edge_mm, 1)
            pe.wait_ge(at_ready, 2)
            walk_t_to_v()
            pe.wait_ge(e_stage, 3)
            accumulate(
                       (banked(p1, 0, 3), window(s3f, 4), blocks(e_t, 0, 3)),
                       (banked(p1, 0, 3), window(s3f, 2), blocks(e_t, 5, 3)),
                       (banked(p1, 0, 1), window(s3f, 0), blocks(e_t, 3, 1)),
                       (banked(p1, 1, 1), window(s3f, 0), blocks(e_t, 1, 1)),
                       (banked(p1, 2, 1), window(s3f, 6), blocks(e_t, 4, 1)),
                       (banked(p1, 1, 1), window(s3f, 6), blocks(e_t, 6, 1)),
                       ).then_inc(edge_mm, 1)

            def turn_ends():
                pe.wait_ge(e_stage, 4)
                pe.wait_ge(ident_ready, 1)
                nc.tensor.transpose(ps_z[1][:, 0:P], e_diff[:, :, :].rearrange("p s b -> p (s b)"),
                                    ident[:, :]).then_inc(turned_mm, 1)

            def sum_w():
                pe.wait_ge(wfold_ready, 1)
                mm(ps_z[0][:, :], ones[:, :], w_fold[:, :], start=True, stop=True).then_inc(wtot_mm, 1)

            def convolve(h):
                for b in range(QUAD):
                    s = h * QUAD + b
                    for g in range(3):
                        last = mm(ps_y[h][:, b * P:(b + 1) * P], x_half[h][:, b, g:g + J],
                                  taps[:, g, :, s, :], start=(g == 0), stop=(g == 2))
                last.then_inc(conv_mm[h], 1)

            def feed_forward(h):
                for q in range(POS):
                    for k, (py, pw) in enumerate(SPLIT):
                        last = mm(ps_z[h][:, :], y_half[h][py][:, q, :, :].rearrange("j b c -> j (b c)"),
                                  w_pair[pw][:, q, :], start=(q == 0 and k == 0), stop=(q == POS - 1 and k == 2))
                last.then_inc(z_mm[h], 1)

            def octet(i, last_octet):
                first_octet = isinstance(i, int) and i == 0
                if not last_octet and not first_octet:
                    pe.wait_ge(at_ready, i + 2)
                    walk_t_to_v()
                pe.wait_ge(ld_x[0], 16 * (i + 1))
                pe.wait_ge(taps_in, 32 * (i + 1))
                pe.wait_ge(taps_moved, 4 * (i + 1))
                convolve(0)
                if first_octet:
                    turn_ends()
                if not last_octet:
                    pe.wait_ge(av_ready, i + 2)
                    walk_v_to_y0()
                if first_octet:
                    pe.wait_ge(lora_added, POS)
                pe.wait_ge(ld_x[1], 16 * (i + 1))
                convolve(1)
                if first_octet:
                    sum_w()
                if not last_octet:
                    pe.wait_ge(ay0_ready, i + 2)
                    walk_y0_to_x()
                for h in range(HALVES):
                    pe.wait_ge(ends_in[h], 32 * (i + 1))
                    if first_octet and h == 0:
                        pe.wait_ge(w_low, POS)
                        pe.wait_ge(wtot_copied, 1)
                    if not first_octet:
                        pe.wait_ge(o_ready[h], i)
                    feed_forward(h)

            octet(0, False)
            with pe.Fori(1, NOCT - 1) as i:
                octet(i, False)
            octet(NOCT - 1, True)


_OUT = (B, C, L)


def kernel(**inputs):
    import concourse.bacc as bacc
    from concourse.bass_utils import run_bass_kernel_spmd

    a = {k: np.asarray(v) for k, v in inputs.items()}
    w = a["L0_cond_weights"]
    rev = w[:, :, :, ::-1]
    kinds = [w[0].transpose(0, 2, 1), w[2].transpose(0, 2, 1), w[1].transpose(0, 2, 1),
             rev[0].transpose(1, 2, 0), rev[1].transpose(1, 2, 0), rev[2].transpose(1, 2, 0),
             rev[3].transpose(1, 2, 0)]
    wpack = np.tile(np.stack(kinds, 1).reshape(C, 7 * K * C), (POS, 1))
    mod = a["L0_cond_mod_w"].transpose(2, 0, 1)
    mod = np.broadcast_to(mod[:, :, None, :], (STYLE, LAYERS, POS, C)).reshape(STYLE, LAYERS * P)
    style = np.concatenate([mod, a["cond_512"].T], 1)
    lw = np.broadcast_to(a["L0_ffn_lora_weights"][:, None], (8, 16)).reshape(P, 1)
    cols = np.concatenate([np.tile(a["L0_cond_mod_b"].T, (POS, 1)), np.tile(a["L0_cond_biases"].T, (POS, 1)), lw], 1)
    x = a["x"]
    blocks = x.reshape(B, C, J, POS).transpose(3, 1, 0, 2).reshape(P, B, J)
    arrays = {
        "wpack": wpack, "style": style, "cols": cols,
        "lora_a": a["L0_ffn_lora_A"].reshape(RANKS, L),
        "lora_b": a["L0_ffn_lora_B"].transpose(0, 2, 1).reshape(RANKS, L),
        "wt": a["L0_ffn_W"].T.reshape(P, POS * L),
        "bias": a["L0_ffn_bias"].reshape(1, L),
        "x_blocks": blocks,
        "x_edges": blocks[:, :, [0, 1, J - 2, J - 1]].transpose(0, 2, 1),
        "x_rows": x.reshape(B * C, L),
    }
    arrays = {k: np.ascontiguousarray(v) for k, v in arrays.items()}
    nc = bacc.Bacc("TRN2", target_bir_lowering=False, num_devices=1)
    args = [nc.dram_tensor(k, v.shape, F32, kind="ExternalInput").ap() for k, v in arrays.items()]
    res = nc.dram_tensor("out", (B * C, L), F32, kind="ExternalOutput").ap()
    build(nc, *args, res)
    r = run_bass_kernel_spmd(nc, [arrays], core_ids=[0])
    return r.results[0]["out"].reshape(_OUT)
```

```python
from contextlib import ExitStack

import numpy as np

import concourse.bass as bass
from concourse import mybir

F32 = mybir.dt.float32
F32R = mybir.dt.float32r
ALU = mybir.AluOpType
ACT = mybir.ActivationFunctionType

B, C, L = 64, 32, 512
LAYERS, K, STYLE = 4, 3, 64
RANKS = 128
P = 128
POS = P // C
J = L // POS
OCT = 8
QUAD = 4
NOCT = B // OCT
HALVES = OCT // QUAD
TAPS = 6
SCALE = 1.0 / float(np.sqrt(C * K ** 2))
LORA_SCALE = 32 / 16
EPS = 1e-8
SPLIT = [(1, 0), (0, 1), (0, 0)]
STACK = len(SPLIT)
BLUR = [1 / 8, 3 / 8, 3 / 8, 1 / 8]
W0T, W2T, W1F, W0F, W1T, W3F, W2F = range(7)


def build(nc, wpack, style, cols, lora_a, lora_b, wt, bias, x_blocks, x_edges, x_rows, out):
    ctx = ExitStack()
    with ctx:
        def sb(name, shape, dtype=F32):
            return ctx.enter_context(nc.sbuf_tensor(name, shape, dtype))

        def pair(name, shape):
            return [sb(f"{name}_hi", shape, F32R), sb(f"{name}_lo", shape, F32R)]

        def pb(name, shape):
            return ctx.enter_context(nc.psum_tensor(name, shape, F32))

        def sem(name):
            return ctx.enter_context(nc.semaphore(name))

        w_sb = sb("w_sb", [P, 7, K * C])
        style_sb = sb("style_sb", [STYLE, LAYERS * P + B])
        cols_sb = sb("cols_sb", [P, 9])
        lora_a_sb = sb("lora_a_sb", [P, J, POS])
        lora_b_sb = sb("lora_b_sb", [P, L])
        w_eff = sb("w_eff", [P, POS, L])
        bias_sb = sb("bias_sb", [P, L])
        x_edge = sb("x_edge", [P, 4, B])
        x_half = [sb(f"x_half{h}", [P, QUAD, J + 2]) for h in range(HALVES)]
        blur1 = sb("blur1", [P, TAPS * C])
        w1_blur = sb("w1_blur", [P, 2, K * C])
        blur1r = sb("blur1r", [P, TAPS * C])
        blur3r = sb("blur3r", [P, TAPS * C])
        s0t = sb("s0t", [P, 8 * C])
        s2t = sb("s2t", [P, 6 * C])
        s1t = sb("s1t", [P, 10 * C])
        s0t_pair = pair("s0t_pair", [P, 8 * C])
        s2t_pair = pair("s2t_pair", [P, 6 * C])
        s1t_pair = pair("s1t_pair", [P, 10 * C])
        s0f = sb("s0f", [P, 12 * C])
        s2f = sb("s2f", [P, 12 * C])
        s1f = sb("s1f", [P, 16 * C])
        s3f = sb("s3f", [P, 10 * C])
        w3_taps = sb("w3_taps", [P, 2, C])
        sty = sb("sty", [P, LAYERS, B])
        sty2 = sb("sty2", [P, LAYERS, B])
        root = sb("root", [P, LAYERS, B])
        root01 = sb("root01", [P, B])
        dem1 = sb("dem1", [P, B])
        dem2 = sb("dem2", [P, B])
        dem3 = sb("dem3", [P, B])
        eps_col = sb("eps_col", [P, 1])
        act_warm = sb("act_warm", [P, 1])
        wsq = sb("wsq", [K * C, LAYERS, POS, C])
        sc_t = sb("sc_t", [P, B])
        sc_v = sb("sc_v", [P, B])
        sc_y0 = sb("sc_y0", [P, B])
        bs_y0 = sb("bs_y0", [P, B])
        bs_v = sb("bs_v", [P, B])
        bs_t = sb("bs_t", [P, B])
        bs_end = sb("bs_end", [P, B])
        out_scale = sb("out_scale", [P, B // QUAD])
        out_const = sb("out_const", [P, B // QUAD])
        const_rep = sb("const_rep", [P, B])
        full_t = sb("full_t", [P, 2, OCT, C])
        full_v = sb("full_v", [P, 2, OCT, C])
        full_y0 = sb("full_y0", [P, 2, OCT, C])
        a_t = pair("a_t", [P, 2, OCT, C])
        a_v = pair("a_v", [P, 2, OCT, C])
        a_y0 = pair("a_y0", [P, 2, OCT, C])
        w_stack1 = sb("w_stack1", [STACK * C, P], F32R)
        w_stack0 = sb("w_stack0", [STACK * C, C], F32R)
        v_stack = sb("v_stack", [STACK * C, OCT, C], F32R)
        y0_stack = sb("y0_stack", [STACK * C, OCT, C], F32R)
        taps = sb("taps", [P, 3, POS, OCT, C])
        e_x = sb("e_x", [P, 4, B])
        e_y0 = sb("e_y0", [P, 7, B])
        e_v = sb("e_v", [P, 8, B])
        e_t = sb("e_t", [P, 8, B])
        e_const = sb("e_const", [P, B])
        e_diff = sb("e_diff", [P, 2, B])
        e_out = sb("e_out", [P, 2, P], F32R)
        ident = sb("ident", [P, P])
        y_half = [sb(f"y_half{h}", [P, 2, POS, QUAD, C], F32R) for h in range(HALVES)]
        w_pair = pair("w_pair", [P, POS, L])
        r_half = [sb(f"r_half{h}", [P, L]) for h in range(HALVES)]
        o_half = [sb(f"o_half{h}", [P, L]) for h in range(HALVES)]
        coef = sb("coef", [P, 1])
        lora_bc = sb("lora_bc", [P, L])
        w_part = sb("w_part", [P, 2, L])
        w_fold = sb("w_fold", [P, L])
        w_total = sb("w_total", [P, L])
        warm = sb("warm", [P, L], F32R)
        ones = sb("ones", [P, P])

        ps_y = [pb(f"ps_y{h}", [P, L]) for h in range(HALVES)]
        ps_z = [pb(f"ps_z{h}", [P, L]) for h in range(HALVES)]
        ps_av = pb("ps_av", [P, L])
        ps_ay0 = pb("ps_ay0", [P, L])
        ps_h = pb("ps_h", [P, L])
        ps_h4 = pb("ps_h4", [P, L])

        LORA_BANK = [ps_h, ps_y[1], ps_ay0, ps_av]

        e_dram = nc.dram_tensor("edge_rows", [2, 2 * POS, B, C], F32, kind="Internal").ap()

        ld_style = sem("ld_style")
        ld_cols = sem("ld_cols")
        ld_w = sem("ld_w")
        ld_xe = sem("ld_xe")
        ld_wt = sem("ld_wt")
        ld_lora_a = sem("ld_lora_a")
        ld_lora_b = sem("ld_lora_b")
        ld_bias = sem("ld_bias")
        ld_x = [sem(f"ld_x{h}") for h in range(HALVES)]
        ld_r = [sem(f"ld_r{h}") for h in range(HALVES)]
        zeroed = sem("zeroed")
        warm_ready = sem("warm_ready")
        taps_zeroed = sem("taps_zeroed")
        ident_zero = sem("ident_zero")
        ident_ready = sem("ident_ready")
        strip_t = sem("strip_t")
        strip_s1t = sem("strip_s1t")
        split_high = sem("split_high")
        split_low = sem("split_low")
        strip_f = sem("strip_f")
        ve = sem("ve")
        coef_ready = sem("coef_ready")
        sty_ready = sem("sty_ready")
        squared2 = sem("squared2")
        sty2_ready = sem("sty2_ready")
        squared = sem("squared")
        blur3_ready = sem("blur3_ready")
        w3_ready = sem("w3_ready")
        blur1_step = sem("blur1_step")
        blur1r_ready = sem("blur1r_ready")
        sty_mm = sem("sty_mm")
        dem_mm = sem("dem_mm")
        rooted = sem("rooted")
        lora_mm = sem("lora_mm")
        lora_added = sem("lora_added")
        w_high = sem("w_high")
        w_low = sem("w_low")
        w_parts = sem("w_parts")
        wfold_ready = sem("wfold_ready")
        wtot_mm = sem("wtot_mm")
        wtot_copied = sem("wtot_copied")
        e_in = sem("e_in")
        edge_mm = sem("edge_mm")
        e_stage = sem("e_stage")
        turned_mm = sem("turned_mm")
        lora_ready = sem("lora_ready")
        e_rows = sem("e_rows")
        edge_written = sem("edge_written")
        at_full = sem("at_full")
        at_high = sem("at_high")
        at_ready = sem("at_ready")
        w_stacked = sem("w_stacked")
        v_stacked_high = sem("v_stacked_high")
        v_stacked_low = sem("v_stacked_low")
        y0_stacked_high = sem("y0_stacked_high")
        y0_stacked_low = sem("y0_stacked_low")
        av_mm = sem("av_mm")
        av_full = sem("av_full")
        av_high = sem("av_high")
        av_ready = sem("av_ready")
        ay0_mm = sem("ay0_mm")
        ay0_full = sem("ay0_full")
        ay0_high = sem("ay0_high")
        ay0_ready = sem("ay0_ready")
        h_mm = sem("h_mm")
        h_ready = sem("h_ready")
        taps_in = sem("taps_in")
        taps_moved = sem("taps_moved")
        conv_mm = [sem(f"conv_mm{h}") for h in range(HALVES)]
        y_high = [sem(f"y_high{h}") for h in range(HALVES)]
        y_low = [sem(f"y_low{h}") for h in range(HALVES)]
        ends_in = [sem(f"ends_in{h}") for h in range(HALVES)]
        z_mm = [sem(f"z_mm{h}") for h in range(HALVES)]
        r_biased = [sem(f"r_biased{h}") for h in range(HALVES)]
        r_const = [sem(f"r_const{h}") for h in range(HALVES)]
        o_ready = [sem(f"o_ready{h}") for h in range(HALVES)]
        stored = [sem(f"stored{h}") for h in range(HALVES)]

        block = ctx.enter_context(nc.Block())

        def window(strip, first, n=POS):
            return strip[:, first * C:(first + n) * C]

        def over_c(t, n=C):
            return t.unsqueeze(2).broadcast_to([P, OCT, n])

        def every_other(t, q, k0):
            return t[q, :].rearrange("c (k o) -> c k o", o=C)[:, k0:min(k0 + 5, TAPS):2, :]

        SQUARED = W0F, W1T, W3F, W2F

        def tap_weights(k, first, n):
            return (w_sb[k * C:(k + 1) * C, SQUARED[first]:SQUARED[first] + n, k * C:(k + 1) * C]
                    .unsqueeze(2).broadcast_to([C, n, POS, C]))

        @block.sync
        def _(sp):
            sp.dma_start(style_sb[:, :], style).then_inc(ld_style, 16)
            sp.dma_start(w_sb[:, :, :].rearrange("p k f -> p (k f)"), wpack).then_inc(ld_w, 16)
            sp.dma_start(x_edge[:, :, :], x_edges).then_inc(ld_xe, 16)
            sp.dma_start(w_eff[:, :, :].rearrange("p q o -> p (q o)"), wt).then_inc(ld_wt, 16)
            sp.wait_ge(zeroed, 1)
            for h in range(HALVES):
                sp.dma_start(x_half[h][:, :, 1:1 + J], x_blocks[:, h * QUAD:(h + 1) * QUAD, :]).then_inc(ld_x[h], 16)
            for h in range(HALVES):
                sp.dma_start(r_half[h][:, :], x_rows[h * P:(h + 1) * P, :]).then_inc(ld_r[h], 16)

            def shift_taps(n):
                sp.wait_ge(h_ready, n + 1)
                sp.dma_start(taps[C:P, :, 1, :, :], taps[0:P - C, :, 0, :, :]).then_inc(taps_in, 16)
                sp.dma_start(taps[0:3 * C, 1:3, 3, :, :], taps[C:P, 0:2, 0, :, :]).then_inc(taps_in, 16)

            shift_taps(0)
            sp.wait_ge(e_rows, 1)
            for side in range(2):
                sp.dma_start(e_dram[side].rearrange("k b c -> b k c"),
                             e_out[side * B:(side + 1) * B, :, :].bitcast(F32)
                             .rearrange("b a (q c) -> b (a q) c", q=POS)).then_inc(edge_written, 16)

            def octet(i, last):
                for h in range(HALVES):
                    sp.wait_ge(y_low[h], i + 1)
                    sp.dma_start(y_half[h][0:P:P - 1, :, :, :, :].bitcast(F32).rearrange("s a q b c -> s (a q) (b c)"),
                                 e_dram[:, :, bass.ds(i * OCT + h * QUAD, QUAD), :].rearrange("s k b c -> s k (b c)")
                                 ).then_inc(ends_in[h], 16)
                    if not last:
                        sp.wait_ge(conv_mm[h], i + 1)
                        sp.dma_start(x_half[h][:, :, 1:1 + J],
                                     x_blocks[:, bass.ds((i + 1) * OCT + h * QUAD, QUAD), :]).then_inc(ld_x[h], 16)
                if not last:
                    shift_taps(i + 1)
                for h in range(HALVES):
                    sp.wait_ge(o_ready[h], i + 1)
                    sp.dma_start(out[bass.ds((i * HALVES + h) * P, P), :], o_half[h][:, :]).then_inc(stored[h], 16)
                    if not last:
                        sp.dma_start(r_half[h][:, :],
                                     x_rows[bass.ds(((i + 1) * HALVES + h) * P, P), :]).then_inc(ld_r[h], 16)

            sp.wait_ge(edge_written, 32)
            with sp.Fori(0, NOCT - 1) as i:
                octet(i, False)
            octet(NOCT - 1, True)
            for h in range(HALVES):
                sp.wait_ge(stored[h], 16 * NOCT)

        @block.gpsimd
        def _(pool):
            nc.gpsimd.memset(warm[:, :].bitcast(F32), 0.0).then_inc(warm_ready, 1)
            nc.gpsimd.memset(ones[:, :], 1.0)
            nc.gpsimd.memset(eps_col[:, :], EPS)
            for t in (blur3r, blur1r, blur1, s2t, s0t, s0f, s1t, s2f, s3f, s1f):
                nc.gpsimd.memset(t[:, :], 0.0)
            for h in range(HALVES):
                last = nc.gpsimd.memset(x_half[h][:, :, 0:J + 2:J + 1], 0.0)
            last.then_inc(zeroed, 1)
            strips = (s2t, s2t_pair), (s0t, s0t_pair), (s1t, s1t_pair)

            def low_strip(k):
                full, (high, low) = strips[k]
                pool.wait_ge(split_high, k + 1)
                nc.gpsimd.tensor_tensor(low[:, :], full[:, :], high[:, :].bitcast(F32),
                                        ALU.subtract).then_inc(split_low, 1)
                pool.wait_ge(split_low, k + 1)

            pool.wait_ge(zeroed, 1)
            pool.wait_ge(ld_w, 16)

            def place(strip, kind):
                for p in range(POS):
                    q = slice(p * C, (p + 1) * C)
                    nc.gpsimd.tensor_copy(strip[q, p * C:(p + K) * C], w_sb[q, kind, :]).then_inc(strip_t, 1)

            for k in range(K):
                w2 = tap_weights(k, 3, 1)[:, 0, :, :]
                nc.gpsimd.tensor_tensor(wsq[k * C:(k + 1) * C, 3, :, :], w2, w2, ALU.mult).then_inc(squared2, 1)
            place(s2t, W2T)
            pool.wait_ge(strip_t, POS)
            pool.wait_ge(ld_xe, 16)
            pool.wait_ge(sty_ready, 1)
            nc.gpsimd.tensor_tensor(e_x[:, :, :], x_edge[:, :, :], sty[:, 0:1, :].broadcast_to([P, 4, B]),
                                    ALU.mult).then_inc(e_in, 1)
            pool.wait_ge(e_in, 1)
            place(s0t, W0T)
            pool.wait_ge(strip_t, 2 * POS)
            for k in range(2):
                nc.gpsimd.tensor_scalar(w1_blur[:, k, :], w_sb[:, W1F, :], 2.0 * BLUR[k], None,
                                        ALU.mult).then_inc(blur1_step, 1)
            pool.wait_ge(blur1_step, 2)
            for j in range(len(BLUR)):
                part = blur1[:, j * C:(j + K) * C]
                nc.gpsimd.tensor_tensor(part, part, w1_blur[:, 1 if j in (1, 2) else 0, :],
                                        ALU.add).then_inc(blur1_step, 1)
                pool.wait_ge(blur1_step, 3 + j)
            nc.gpsimd.memset(taps[:, 2, 0, :, :], 0.0)
            nc.gpsimd.memset(taps[:, 0, :, :, :], 0.0).then_inc(taps_zeroed, 1)
            pool.wait_ge(taps_zeroed, 1)
            low_strip(0)
            low_strip(1)
            low_strip(2)
            nc.gpsimd.memset(ident[:, :], 0.0).then_inc(ident_zero, 1)
            pool.wait_ge(ident_zero, 1)
            nc.gpsimd.affine_select(out=ident[:, :], in_=ident[:, :], compare_op=ALU.not_equal, fill=1.0, base=0,
                                    pattern=[[-1, P]], channel_multiplier=1).then_inc(ident_ready, 1)
            pool.wait_ge(ident_ready, 1)
            for q in range(POS):
                pool.wait_ge(w_high, q + 1)
                nc.gpsimd.tensor_tensor(w_pair[1][:, q, :], w_eff[:, q, :], w_pair[0][:, q, :].bitcast(F32),
                                        ALU.subtract).then_inc(w_low, 1)
                pool.wait_ge(w_low, q + 1)
            pool.wait_ge(lora_added, POS)
            for k in range(2):
                nc.gpsimd.tensor_tensor(w_part[:, k, :], w_eff[:, 2 * k, :], w_eff[:, 2 * k + 1, :],
                                        ALU.add).then_inc(w_parts, 1)
                pool.wait_ge(w_parts, k + 1)
            nc.gpsimd.tensor_tensor(w_fold[:, :], w_part[:, 0, :], w_part[:, 1, :], ALU.add).then_inc(wfold_ready, 1)
            pool.wait_ge(wfold_ready, 1)
            pool.wait_ge(ld_bias, 16)

            def octet(i):
                for h in range(HALVES):
                    pool.wait_ge(ld_r[h], 16 * (i + 1))
                    nc.gpsimd.tensor_tensor(r_half[h][:, :], r_half[h][:, :], bias_sb[:, :],
                                            ALU.add).then_inc(r_biased[h], 1)
                    pool.wait_ge(r_biased[h], i + 1)

            with pool.Fori(0, NOCT) as i:
                octet(i)

        @block.scalar
        def _(act):
            act.dma_start(cols_sb[:, :], cols).then_inc(ld_cols, 16)
            act.dma_start(lora_b_sb[:, :], lora_b).then_inc(ld_lora_b, 16)
            act.dma_start(lora_a_sb[:, :, :].rearrange("r j q -> r (j q)"), lora_a).then_inc(ld_lora_a, 16)
            act.dma_start(bias_sb[:, :], bias.broadcast_to([P, L])).then_inc(ld_bias, 16)
            act.wait_ge(zeroed, 1)
            nc.scalar.activation(act_warm[:, :], eps_col[:, :], ACT.Sqrt)
            act.wait_ge(ld_cols, 16)
            nc.scalar.mul(coef[:, :], cols_sb[:, 8:9], LORA_SCALE).then_inc(coef_ready, 1)
            act.wait_ge(coef_ready, 1)
            act.wait_ge(ld_lora_b, 16)
            nc.scalar.activation(lora_bc[:, :], lora_b_sb[:, :], ACT.Copy, scale=coef[:, 0:1]).then_inc(lora_ready, 1)

            def place(strip, at, src, n):
                for p in range(POS):
                    q = slice(p * C, (p + 1) * C)
                    nc.scalar.activation(strip[q, at(p) * C:(at(p) + n) * C].rearrange("c (k o) -> c k o", o=C),
                                         src(p, q), ACT.Copy).then_inc(strip_f, 1)

            def shift_taps(n):
                act.wait_ge(h_ready, n + 1)
                for q, rows, src, blocks in ((2, slice(64, P), slice(0, 64), slice(0, 3)),
                                             (2, slice(0, 64), slice(64, P), slice(1, 3)),
                                             (3, slice(96, P), slice(0, 32), slice(0, 3)),
                                             (1, slice(0, 32), slice(96, P), slice(1, 3))):
                    before = slice(blocks.start - 1, blocks.stop - 1) if blocks.start else blocks
                    nc.scalar.activation(taps[rows, blocks, q, :, :].rearrange("p g b c -> p g (b c)"),
                                         taps[src, before, 0, :, :].rearrange("p g b c -> p g (b c)"),
                                         ACT.Copy).then_inc(taps_moved, 1)

            def high(full, parts, full_sem, high_sem, n):
                act.wait_ge(full_sem, n + 1)
                nc.scalar.activation(parts[0][:, :, :, :], full[:, :, :, :], ACT.Copy).then_inc(high_sem, 1)

            def high_stack(full, stack, stacked, slot, p):
                for k in (0, 2):
                    nc.scalar.activation(stack[k * C:(k + 1) * C, :, :], full[p * C:(p + 1) * C, slot, :, :],
                                         ACT.Copy).then_inc(stacked, 1)

            def stack_weights():
                act.wait_ge(split_low, 3)
                for stack, strip, first, p in ((w_stack1, s1t_pair, 6, 3), (w_stack0, s0t_pair, 4, 2)):
                    for k, (pw, _) in enumerate(SPLIT):
                        nc.scalar.activation(stack[k * C:(k + 1) * C, :],
                                             strip[pw][p * C:(p + 1) * C, first * C:first * C + stack.shape[1]]
                                             .bitcast(F32), ACT.Copy).then_inc(w_stacked, 1)

            def high_w(q):
                act.wait_ge(lora_added, q + 1)
                nc.scalar.activation(w_pair[0][:, q, :], w_eff[:, q, :], ACT.Copy).then_inc(w_high, 1)

            def square(k):
                nc.scalar.activation(wsq[k * C:(k + 1) * C, 0:3, :, :], tap_weights(k, 0, 3),
                                     ACT.Square).then_inc(squared, 1)

            act.wait_ge(blur3_ready, 1)
            for p in range(POS):
                q = slice(p * C, (p + 1) * C)
                nc.scalar.activation(w3_taps[q, :, :],
                                     blur3r[q, :].rearrange("c (k o) -> c k o", o=C)[:, 3 - p:6 - p:2, :],
                                     ACT.Copy).then_inc(w3_ready, 1)
            act.wait_ge(dem_mm, 1)
            nc.scalar.activation(root[:, 2, :], ps_av[:, 2 * B:3 * B], ACT.Sqrt, bias=eps_col[:, :]).then_inc(rooted, 1)
            act.wait_ge(ld_w, 16)
            square(0)
            square(1)
            square(2)
            place(s0f, lambda p: p + 3, lambda p, q: w_sb[q, W0F, :].rearrange("c (k o) -> c k o", o=C), K)
            act.wait_ge(blur1r_ready, 1)
            for p in range(POS):
                q = slice(p * C, (p + 1) * C)
                first = {0: -2, 1: -1, 2: -1, 3: 0}[p]
                nc.scalar.activation(s1t[q, (first + 4) * C:(first + 7) * C].rearrange("c (k o) -> c k o", o=C),
                                     every_other(blur1r, q, 4 - p + 2 * first), ACT.Copy).then_inc(strip_s1t, 1)
            act.wait_ge(dem_mm, 2)
            nc.scalar.activation(root[:, 0:2, :].rearrange("p l b -> p (l b)"), ps_z[1][:, 0:2 * B],
                                 ACT.Sqrt, bias=eps_col[:, :])
            nc.scalar.activation(root[:, 3, :], ps_z[1][:, 3 * B:4 * B], ACT.Sqrt,
                                 bias=eps_col[:, :]).then_inc(rooted, 1)
            act.wait_ge(blur1_step, 2 + len(BLUR))
            place(s1f, lambda p: 2 * p + 2, lambda p, q: blur1[q, :].rearrange("c (k o) -> c k o", o=C), TAPS)
            act.wait_ge(strip_t, POS)
            nc.scalar.activation(s2t_pair[0][:, :], s2t[:, :], ACT.Copy).then_inc(split_high, 1)
            place(s2f, lambda p: p + 3, lambda p, q: w_sb[q, W2F, :].rearrange("c (k o) -> c k o", o=C), K)
            act.wait_ge(strip_t, 2 * POS)
            nc.scalar.activation(s0t_pair[0][:, :], s0t[:, :], ACT.Copy).then_inc(split_high, 1)
            act.wait_ge(strip_s1t, POS)
            nc.scalar.activation(s1t_pair[0][:, :], s1t[:, :], ACT.Copy).then_inc(split_high, 1)
            place(s3f, lambda p: p // 2 + 3, lambda p, q: every_other(blur3r, q, 3 - p + 2 * (p // 2 - 1)), 3)
            high_w(0)
            high_w(1)
            shift_taps(0)
            high_w(2)
            high(full_t, a_t, at_full, at_high, 1)
            stack_weights()
            high_w(3)
            high(full_v, a_v, av_full, av_high, 1)
            high_stack(full_v, v_stack, v_stacked_high, 0, 3)

            def octet(i, walk=True, start=True):
                first = isinstance(i, int) and i == 0
                for h in range(HALVES):
                    act.wait_ge(conv_mm[h], i + 1)
                    if not first:
                        act.wait_ge(z_mm[h], i)
                    nc.scalar.activation(y_half[h][:, 0, :, :, :].rearrange("j q b c -> j b q c"),
                                         ps_y[h][:, :].rearrange("j (b q c) -> j b q c", b=QUAD, q=POS),
                                         ACT.Copy).then_inc(y_high[h], 1)
                    if h == 0 and walk:
                        high(full_y0, a_y0, ay0_full, ay0_high, i + 1)
                        high_stack(full_y0, y0_stack, y0_stacked_high, 1, 2)
                if start:
                    high(full_t, a_t, at_full, at_high, i + 2)
                if walk:
                    shift_taps(i + 1)
                if start:
                    high(full_v, a_v, av_full, av_high, i + 2)
                    high_stack(full_v, v_stack, v_stacked_high, 0, 3)

            octet(0)
            with act.Fori(1, NOCT - 2) as i:
                octet(i)
            octet(NOCT - 2, start=False)
            octet(NOCT - 1, walk=False, start=False)

        @block.vector
        def _(dve):
            done = [0]

            def link(ins):
                done[0] += 1
                ins.then_inc(ve, 1)
                dve.wait_ge(ve, done[0])

            V = nc.vector
            def blur(j, *kernels, signal=None):
                for dst, kind, gain in kernels:
                    part = dst[:, j * C:(j + K) * C]
                    last = V.scalar_tensor_tensor(part, w_sb[:, kind, :], gain * BLUR[j], part, ALU.mult, ALU.add)
                if signal is None:
                    link(last)
                else:
                    last.then_inc(signal, 1)

            dve.wait_ge(zeroed, 1)
            dve.wait_ge(ld_w, 16)
            for j in range(len(BLUR) - 1):
                blur(j, (blur3r, W3F, 1.0))
            blur(3, (blur3r, W3F, 1.0), signal=blur3_ready)
            dve.wait_ge(sty_mm, 1)
            dve.wait_ge(ld_cols, 16)

            def styles(l):
                return V.tensor_scalar(sty[:, l, :], ps_z[0][:, l * B:(l + 1) * B], cols_sb[:, l:l + 1], SCALE,
                                       ALU.add, ALU.mult)

            link(styles(2))
            V.tensor_tensor(sty2[:, 2, :], sty[:, 2, :], sty[:, 2, :], ALU.mult).then_inc(sty2_ready, 1)
            styles(0)
            styles(3)
            styles(1).then_inc(sty_ready, 1)
            dve.wait_ge(rooted, 1)
            link(V.reciprocal(dem2[:, :], root[:, 2, :]))
            link(V.tensor_tensor(sc_t[:, :], sty[:, 3, :], dem2[:, :], ALU.mult))

            def start_taps(col):
                for slot in range(2):
                    last = V.tensor_tensor(full_t[:, slot, :, :],
                                           w3_taps[:, slot, :].unsqueeze(1).broadcast_to([P, OCT, C]),
                                           over_c(sc_t[:, col]), ALU.mult)
                last.then_inc(at_full, 1)

            def low_stack(full, parts, stack, stacked, slot, p):
                V.tensor_tensor(stack[C:2 * C, :, :], full[p * C:(p + 1) * C, slot, :, :],
                                parts[0][p * C:(p + 1) * C, slot, :, :].bitcast(F32), ALU.subtract).then_inc(stacked, 1)

            def low(full, parts, high_sem, ready, n):
                dve.wait_ge(high_sem, n)
                V.tensor_tensor(parts[1][:, :, :, :], full[:, :, :, :], parts[0][:, :, :, :].bitcast(F32),
                                ALU.subtract).then_inc(ready, 1)

            dve.wait_ge(w3_ready, POS)
            start_taps(slice(0, OCT))
            for layers in (slice(0, 2), slice(3, 4)):
                last = V.tensor_tensor(sty2[:, layers, :], sty[:, layers, :], sty[:, layers, :], ALU.mult)
            last.then_inc(sty2_ready, 1)
            blur(0, (blur1r, W1T, 2.0))
            V.tensor_tensor(sc_v[:, :], sty[:, 2, :], sty[:, 1, :], ALU.mult)
            blur(1, (blur1r, W1T, 2.0))
            V.tensor_scalar(bs_t[:, :], sty[:, 3, :], cols_sb[:, 6:7], None, ALU.mult)
            blur(2, (blur1r, W1T, 2.0))
            V.tensor_scalar(bs_v[:, :], sty[:, 2, :], cols_sb[:, 5:6], 2.0, ALU.mult, ALU.mult)
            blur(3, (blur1r, W1T, 2.0), signal=blur1r_ready)
            V.tensor_scalar(bs_end[:, :], sty[:, 2, :], cols_sb[:, 5:6], -2.0 * BLUR[0], ALU.mult, ALU.mult)

            def scale_av(col):
                V.tensor_tensor(full_v[:, :, :, :], ps_av[:, :].rearrange("p (s b c) -> p s b c", s=2, b=OCT),
                                sc_v[:, col].unsqueeze(1).unsqueeze(3).broadcast_to([P, 2, OCT, C]),
                                ALU.mult).then_inc(av_full, 1)

            def scale_ay0(col):
                V.tensor_tensor(full_y0[:, :, :, :], ps_ay0[:, :].rearrange("p (s b c) -> p s b c", s=2, b=OCT),
                                sc_y0[:, col].unsqueeze(1).unsqueeze(3).broadcast_to([P, 2, OCT, C]),
                                ALU.mult).then_inc(ay0_full, 1)

            def scale_h(col):
                V.tensor_tensor(taps[:, 0:2, 0, :, :], ps_h[:, :].rearrange("p (s b c) -> p s b c", s=2, b=OCT),
                                sty[:, 0, col].unsqueeze(1).unsqueeze(3).broadcast_to([P, 2, OCT, C]), ALU.mult)
                V.tensor_tensor(taps[0:C, 2, 0, :, :], ps_h4[0:C, 0:OCT * C].rearrange("p (b c) -> p b c", b=OCT),
                                sty[0:C, 0, col].unsqueeze(2).broadcast_to([C, OCT, C]),
                                ALU.mult).then_inc(h_ready, 1)

            def add_lora(q):
                dve.wait_ge(lora_mm, q + 1)
                dve.wait_ge(ld_wt, 16)
                V.tensor_tensor(w_eff[:, q, :], w_eff[:, q, :], LORA_BANK[q][:, :], ALU.add).then_inc(lora_added, 1)

            dve.wait_ge(av_mm, 1)
            scale_av(slice(0, OCT))
            add_lora(0)
            dve.wait_ge(rooted, 2)
            link(V.tensor_tensor(root01[:, :], root[:, 0, :], root[:, 1, :], ALU.mult))
            V.reciprocal(dem1[:, :], root[:, 1, :])
            link(V.reciprocal(sc_y0[:, :], root01[:, :]))
            link(V.tensor_scalar(bs_y0[:, :], dem1[:, :], cols_sb[:, 4:5], None, ALU.mult))
            V.tensor_copy(e_y0[:, 0:7:3, :], bs_y0[:, :].unsqueeze(1).broadcast_to([P, 3, B]))
            dve.wait_ge(ay0_mm, 1)
            scale_ay0(slice(0, OCT))
            dve.wait_ge(edge_mm, 1)
            two = [P, 2, B]
            y0_left, y0_right = e_y0[:, 2:6:3, :], e_y0[:, 1:5:3, :]
            for k, dst in ((0, y0_left), (1, y0_right)):
                last = V.tensor_tensor(dst, ps_y[0][:, 2 * k * B:2 * (k + 1) * B].rearrange("p (k b) -> p k b", b=B),
                                       sc_y0[:, :].unsqueeze(1).broadcast_to(two), ALU.mult)
            link(last)
            for dst in (y0_left, y0_right):
                last = V.tensor_tensor(dst, dst, bs_y0[:, :].unsqueeze(1).broadcast_to(two), ALU.add)
            last.then_inc(e_stage, 1)
            add_lora(1)

            def end_stage(dst, src, scale, shift):
                eight = [P, 8, B]
                link(V.tensor_tensor(dst[:, :, :], src[:, :].rearrange("p (k b) -> p k b", b=B),
                                     scale[:, :].unsqueeze(1).broadcast_to(eight), ALU.mult))
                return V.tensor_tensor(dst[:, :, :], dst[:, :, :], shift[:, :].unsqueeze(1).broadcast_to(eight),
                                       ALU.add)

            dve.wait_ge(h_mm, 1)
            dve.wait_ge(taps_zeroed, 1)
            scale_h(slice(0, OCT))
            dve.wait_ge(edge_mm, 2)
            link(end_stage(e_v, ps_z[0], sc_v, bs_v))
            V.tensor_tensor(e_v[0:C, 0, :], e_v[0:C, 0, :], bs_end[0:C, :], ALU.add)
            V.tensor_tensor(e_v[P - C:P, 7, :], e_v[P - C:P, 7, :], bs_end[P - C:P, :],
                            ALU.add).then_inc(e_stage, 1)
            start_taps(slice(OCT, 2 * OCT))
            add_lora(2)
            dve.wait_ge(edge_mm, 3)
            end_stage(e_t, ps_z[1], sc_t, bs_t).then_inc(e_stage, 1)
            low(full_t, a_t, at_high, at_ready, 1)
            add_lora(3)
            V.reciprocal(dem3[:, :], root[:, 3, :])
            dve.wait_ge(edge_mm, 4)
            link(V.tensor_copy(e_const[:, :], ps_z[0][:, B:2 * B]))
            V.tensor_tensor(e_diff[:, :, :], ps_z[0][:, 0:3 * B].rearrange("p (k b) -> p k b", b=B)[:, 0:3:2, :],
                            e_const[:, :].unsqueeze(1).broadcast_to(two), ALU.subtract).then_inc(e_stage, 1)
            link(V.tensor_tensor(const_rep[:, :], e_const[:, :], dem3[:, :], ALU.mult))
            dve.wait_ge(av_mm, 2)
            scale_av(slice(OCT, 2 * OCT))
            dve.wait_ge(turned_mm, 1)
            link(V.tensor_copy(e_out[:, 0, :], ps_z[1][:, 0:P]))
            V.tensor_tensor(e_out[:, 1, :], ps_z[1][:, 0:P], e_out[:, 0, :].bitcast(F32),
                            ALU.subtract).then_inc(e_rows, 1)
            low(full_v, a_v, av_high, av_ready, 1)
            low_stack(full_v, a_v, v_stack, v_stacked_low, 0, 3)
            for r in range(QUAD):
                q = slice(r * C, (r + 1) * C)
                V.tensor_copy(out_scale[q, :], dem3[q, r:B:QUAD])
                last = V.tensor_scalar(out_const[q, :], const_rep[q, r:B:QUAD], cols_sb[q, 7:8], None, ALU.add)
            link(last)

            def copy_w_total():
                dve.wait_ge(wtot_mm, 1)
                V.tensor_copy(w_total[:, :], ps_z[0][:, :]).then_inc(wtot_copied, 1)
                dve.wait_ge(wtot_copied, 1)

            def octet(i, walk=True, start=True):
                def col(n):
                    return slice(n * OCT, (n + 1) * OCT) if isinstance(n, int) else bass.ds(n * OCT, OCT)

                def row(t, h):
                    return t[:, bass.ds(i * HALVES + h, 1)]

                def add_const(h):
                    dve.wait_ge(r_biased[h], i + 1)
                    V.scalar_tensor_tensor(r_half[h][:, :], w_total[:, :], row(out_const, h), r_half[h][:, :],
                                           ALU.mult, ALU.add).then_inc(r_const[h], 1)

                def y_low_part(h):
                    dve.wait_ge(y_high[h], i + 1)
                    V.tensor_tensor(y_half[h][:, 1, :, :, :].rearrange("j q b c -> j b q c"),
                                    ps_y[h][:, :].rearrange("j (b q c) -> j b q c", b=QUAD, q=POS),
                                    y_half[h][:, 0, :, :, :].bitcast(F32).rearrange("j q b c -> j b q c"),
                                    ALU.subtract).then_inc(y_low[h], 1)

                first = isinstance(i, int) and i == 0
                y_low_part(0)
                if walk:
                    dve.wait_ge(ay0_mm, i + 2)
                    scale_ay0(col(i + 1))
                    low(full_y0, a_y0, ay0_high, ay0_ready, i + 1)
                    low_stack(full_y0, a_y0, y0_stack, y0_stacked_low, 1, 2)
                if start and not first:
                    start_taps(col(i + 2))
                if first:
                    copy_w_total()
                y_low_part(1)
                if first:
                    start_taps(col(i + 2))
                if walk:
                    dve.wait_ge(h_mm, i + 2)
                    scale_h(col(i + 1))
                if start:
                    low(full_t, a_t, at_high, at_ready, i + 2)
                for h in range(HALVES):
                    add_const(h)
                for h in range(HALVES):
                    dve.wait_ge(z_mm[h], i + 1)
                    dve.wait_ge(r_const[h], i + 1)
                    if not (isinstance(i, int) and i == 0):
                        dve.wait_ge(stored[h], 16 * i)
                    V.scalar_tensor_tensor(o_half[h][:, :], ps_z[h][:, :], row(out_scale, h), r_half[h][:, :],
                                           ALU.mult, ALU.add).then_inc(o_ready[h], 1)
                    if start and h == 0:
                        dve.wait_ge(av_mm, i + 3)
                        scale_av(col(i + 2))
                        low(full_v, a_v, av_high, av_ready, i + 2)
                        low_stack(full_v, a_v, v_stack, v_stacked_low, 0, 3)

            octet(0)
            with dve.Fori(1, NOCT - 2) as i:
                octet(i)
            octet(NOCT - 2, start=False)
            octet(NOCT - 1, walk=False, start=False)

        @block.tensor
        def _(pe):
            mm = nc.tensor.matmul

            def keep_warm(n):
                for _ in range(n):
                    mm(ps_ay0[:, :], warm[:, 0:P], warm[:, :], start=True, stop=True)

            pe.wait_ge(warm_ready, 1)
            keep_warm(5)
            pe.wait_ge(ld_style, 16)
            for l in range(LAYERS):
                last = mm(ps_z[0][:, l * B:(l + 1) * B], style_sb[:, l * P:(l + 1) * P],
                          style_sb[:, LAYERS * P:], start=True, stop=True)
            last.then_inc(sty_mm, 1)
            def lora(q):
                mm(LORA_BANK[q][:, :], lora_a_sb[:, :, q], lora_bc[:, :],
                   start=True, stop=True).then_inc(lora_mm, 1)

            keep_warm(3)
            pe.wait_ge(squared2, K)
            pe.wait_ge(sty2_ready, 1)

            def sum_squares(dst, l, at):
                return mm(dst[:, l * B:(l + 1) * B], wsq[:, at, :, :].rearrange("i r o -> i (r o)"),
                          sty2[0:K * C, l, :], start=True, stop=True)

            sum_squares(ps_av, 2, 3).then_inc(dem_mm, 1)
            pe.wait_ge(lora_ready, 1)
            pe.wait_ge(ld_lora_a, 16)
            lora(0)
            keep_warm(1)

            def walk(dst, *terms):
                passes = [(strip[pw], first, state[pm], slot) for strip, first, state, slot in terms
                          for pw, pm in (SPLIT if len(strip) == 2 else [(0, 0)])]
                for k, (strip, first, state, slot) in enumerate(passes):
                    last = mm(dst, window(strip, first), state[:, slot, :, :].rearrange("p b c -> p (b c)"),
                              start=(k == 0), stop=(k == len(passes) - 1))
                return last

            one, two = slice(0, OCT * C), slice(OCT * C, 2 * OCT * C)

            def walk_t_to_v(s2t_pair=s2t_pair, a_t=a_t):
                walk(ps_av[:, one], (s2t_pair, 0, a_t, 1))
                walk(ps_av[:, two], (s2t_pair, 2, a_t, 0)).then_inc(av_mm, 1)

            def walk_v_to_y0(n):
                walk(ps_ay0[:, one], (s1t_pair, 2, a_v, 0), (s1t_pair, 0, a_v, 1))
                for k, (pw, pm) in enumerate(SPLIT):
                    mm(ps_ay0[:, two], window(s1t_pair[pw], 4), a_v[pm][:, 1, :, :].rearrange("p b c -> p (b c)"),
                       start=(k == 0), stop=False)
                pe.wait_ge(v_stacked_high, 2 * n)
                pe.wait_ge(v_stacked_low, n)
                mm(ps_ay0[:, two], w_stack1[:, :], v_stack[:, :, :].rearrange("p b c -> p (b c)"),
                   start=False, stop=True).then_inc(ay0_mm, 1)

            def walk_y0_to_x(n):
                walk(ps_h[:, one], (s0t_pair, 0, a_y0, 0))
                walk(ps_h[:, two], (s0t_pair, 4, a_y0, 0), (s0t_pair, 0, a_y0, 1))
                pe.wait_ge(y0_stacked_high, 2 * n)
                pe.wait_ge(y0_stacked_low, n)
                mm(ps_h4[0:C, one], w_stack0[:, :], y0_stack[:, :, :].rearrange("p b c -> p (b c)"),
                   start=True, stop=True).then_inc(h_mm, 1)

            def accumulate(*terms):
                for k, (dst, w, m) in enumerate(terms):
                    last = mm(dst, w, m, start=(k == 0), stop=(k == len(terms) - 1))
                return last

            def blocks(t, first, n, step=1):
                return t[:, first:first + (n - 1) * step + 1:step, :]

            def banked(ps, first, n, step=1):
                return blocks(ps[:, :].rearrange("p (k b) -> p k b", b=B), first, n, step)

            pe.wait_ge(strip_t, POS)
            pe.wait_ge(at_full, 1)
            walk_t_to_v([s2t], [full_t])
            pe.wait_ge(squared, K)
            pe.wait_ge(sty2_ready, 2)
            for at, l in enumerate((0, 1, 3)):
                last = sum_squares(ps_z[1], l, at)
            last.then_inc(dem_mm, 1)
            pe.wait_ge(strip_f, POS)
            pe.wait_ge(e_in, 1)
            p0 = ps_y[0]
            accumulate((banked(p0, 0, 4), window(s0f, 4), blocks(e_x, 0, 4)),
                       (banked(p0, 0, 2, 2), window(s0f, 0), blocks(e_x, 1, 2, 2)),
                       (banked(p0, 1, 2, 2), window(s0f, 8), blocks(e_x, 0, 2, 2))).then_inc(edge_mm, 1)
            pe.wait_ge(av_full, 1)
            pe.wait_ge(strip_s1t, POS)
            walk(ps_ay0[:, one], ([s1t], 2, [full_v], 0), ([s1t], 0, [full_v], 1))
            walk(ps_ay0[:, two], ([s1t], 6, [full_v], 0), ([s1t], 4, [full_v], 1)).then_inc(ay0_mm, 1)
            lora(1)
            pe.wait_ge(ay0_full, 1)
            pe.wait_ge(lora_added, 1)
            pe.wait_ge(strip_t, 2 * POS)
            walk(ps_h4[:, one], ([s0t], 4, [full_y0], 1))
            walk(ps_h[:, one], ([s0t], 0, [full_y0], 0))
            walk(ps_h[:, two], ([s0t], 4, [full_y0], 0), ([s0t], 0, [full_y0], 1)).then_inc(h_mm, 1)
            pe.wait_ge(e_stage, 1)
            pe.wait_ge(strip_f, 2 * POS)
            p1 = ps_z[0]
            accumulate((banked(p1, 0, 4), window(s1f, 4), blocks(e_y0, 2, 4)),
                       (banked(p1, 1, 3), window(s1f, 12), blocks(e_y0, 0, 3)))
            accumulate((banked(p1, 4, 4), window(s1f, 8), blocks(e_y0, 1, 4)),
                       (banked(p1, 4, 3), window(s1f, 0), blocks(e_y0, 4, 3))).then_inc(edge_mm, 1)
            lora(2)
            lora(3)
            pe.wait_ge(e_stage, 2)
            pe.wait_ge(strip_f, 3 * POS)
            p2 = ps_z[1]
            accumulate((banked(p2, 0, 8), window(s2f, 4), blocks(e_v, 0, 8)),
                       (banked(p2, 0, 3), window(s2f, 0), blocks(e_v, 5, 3)),
                       (banked(p2, 5, 3), window(s2f, 8), blocks(e_v, 0, 3)),
                       (banked(p2, 4, 2), window(s2f, 0), blocks(e_v, 2, 2)),
                       (banked(p2, 2, 2), window(s2f, 8), blocks(e_v, 4, 2)),
                       (banked(p2, 6, 1), window(s2f, 0), blocks(e_v, 1, 1)),
                       (banked(p2, 1, 1), window(s2f, 8), blocks(e_v, 6, 1)),
                       ).then_inc(edge_mm, 1)
            def end_stage_3():
                pe.wait_ge(e_stage, 3)
                pe.wait_ge(strip_f, 4 * POS)
                accumulate(
                           (banked(p1, 0, 3), window(s3f, 4), blocks(e_t, 0, 3)),
                           (banked(p1, 0, 3), window(s3f, 2), blocks(e_t, 5, 3)),
                           (banked(p1, 0, 1), window(s3f, 0), blocks(e_t, 3, 1)),
                           (banked(p1, 1, 1), window(s3f, 0), blocks(e_t, 1, 1)),
                           (banked(p1, 2, 1), window(s3f, 6), blocks(e_t, 4, 1)),
                           (banked(p1, 1, 1), window(s3f, 6), blocks(e_t, 6, 1)),
                           ).then_inc(edge_mm, 1)

            def turn_ends():
                pe.wait_ge(e_stage, 4)
                pe.wait_ge(ident_ready, 1)
                nc.tensor.transpose(ps_z[1][:, 0:P], e_diff[:, :, :].rearrange("p s b -> p (s b)"),
                                    ident[:, :]).then_inc(turned_mm, 1)

            def sum_w():
                pe.wait_ge(wfold_ready, 1)
                mm(ps_z[0][:, :], ones[:, :], w_fold[:, :], start=True, stop=True).then_inc(wtot_mm, 1)

            def convolve(h, samples=range(QUAD)):
                for b in samples:
                    s = h * QUAD + b
                    for g in range(3):
                        last = mm(ps_y[h][:, b * P:(b + 1) * P], x_half[h][:, b, g:g + J],
                                  taps[:, g, :, s, :], start=(g == 0), stop=(g == 2))
                if b == QUAD - 1:
                    last.then_inc(conv_mm[h], 1)

            def feed_forward(h):
                for q in range(POS):
                    for k, (py, pw) in enumerate(SPLIT):
                        last = mm(ps_z[h][:, :], y_half[h][:, py, q, :, :].rearrange("j b c -> j (b c)"),
                                  w_pair[pw][:, q, :], start=(q == 0 and k == 0), stop=(q == POS - 1 and k == 2))
                last.then_inc(z_mm[h], 1)

            def octet(i, walk=True, start=True):
                first_octet = isinstance(i, int) and i == 0
                pe.wait_ge(ld_x[0], 16 * (i + 1))
                pe.wait_ge(taps_in, 32 * (i + 1))
                pe.wait_ge(taps_moved, 4 * (i + 1))
                if first_octet:
                    convolve(0, range(QUAD - 1))
                    end_stage_3()
                    pe.wait_ge(split_low, 3)
                    pe.wait_ge(at_ready, 1)
                    pe.wait_ge(lora_added, POS)
                    walk_t_to_v()
                    turn_ends()
                    convolve(0, [QUAD - 1])
                    pe.wait_ge(ld_x[1], 16)
                    convolve(1, range(QUAD // 2))
                else:
                    convolve(0)
                if walk:
                    pe.wait_ge(av_ready, i + 1)
                    if first_octet:
                        pe.wait_ge(w_stacked, 2 * STACK)
                    walk_v_to_y0(i + 1)
                if first_octet:
                    convolve(1, range(QUAD // 2, QUAD))
                    sum_w()
                else:
                    pe.wait_ge(ld_x[1], 16 * (i + 1))
                    convolve(1)
                if walk:
                    pe.wait_ge(ay0_ready, i + 1)
                    walk_y0_to_x(i + 1)
                for h in range(HALVES):
                    pe.wait_ge(ends_in[h], 16 * (i + 1))
                    if first_octet and h == 0:
                        pe.wait_ge(w_low, POS)
                        pe.wait_ge(wtot_copied, 1)
                    if not first_octet:
                        pe.wait_ge(o_ready[h], i)
                    feed_forward(h)
                    if start and h == 0:
                        pe.wait_ge(at_ready, i + 2)
                        walk_t_to_v()

            octet(0)
            with pe.Fori(1, NOCT - 2) as i:
                octet(i)
            octet(NOCT - 2, start=False)
            octet(NOCT - 1, walk=False, start=False)


_OUT = (B, C, L)


def kernel(**inputs):
    import concourse.bacc as bacc
    from concourse.bass_utils import run_bass_kernel_spmd

    a = {k: np.asarray(v) for k, v in inputs.items()}
    w = a["L0_cond_weights"]
    rev = w[:, :, :, ::-1]
    kinds = [w[0].transpose(0, 2, 1), w[2].transpose(0, 2, 1), w[1].transpose(0, 2, 1),
             rev[0].transpose(1, 2, 0), rev[1].transpose(1, 2, 0), rev[3].transpose(1, 2, 0),
             rev[2].transpose(1, 2, 0)]
    wpack = np.tile(np.stack(kinds, 1).reshape(C, 7 * K * C), (POS, 1))
    mod = a["L0_cond_mod_w"].transpose(2, 0, 1)
    mod = np.broadcast_to(mod[:, :, None, :], (STYLE, LAYERS, POS, C)).reshape(STYLE, LAYERS * P)
    style = np.concatenate([mod, a["cond_512"].T], 1)
    lw = np.broadcast_to(a["L0_ffn_lora_weights"][:, None], (8, 16)).reshape(P, 1)
    cols = np.concatenate([np.tile(a["L0_cond_mod_b"].T, (POS, 1)), np.tile(a["L0_cond_biases"].T, (POS, 1)), lw], 1)
    x = a["x"]
    blocks = x.reshape(B, C, J, POS).transpose(3, 1, 0, 2).reshape(P, B, J)
    arrays = {
        "wpack": wpack, "style": style, "cols": cols,
        "lora_a": a["L0_ffn_lora_A"].reshape(RANKS, L),
        "lora_b": a["L0_ffn_lora_B"].transpose(0, 2, 1).reshape(RANKS, L),
        "wt": a["L0_ffn_W"].T.reshape(P, POS * L),
        "bias": a["L0_ffn_bias"].reshape(1, L),
        "x_blocks": blocks,
        "x_edges": blocks[:, :, [0, 1, J - 2, J - 1]].transpose(0, 2, 1),
        "x_rows": x.reshape(B * C, L),
    }
    arrays = {k: np.ascontiguousarray(v) for k, v in arrays.items()}
    nc = bacc.Bacc("TRN2", target_bir_lowering=False, num_devices=1)
    args = [nc.dram_tensor(k, v.shape, F32, kind="ExternalInput").ap() for k, v in arrays.items()]
    res = nc.dram_tensor("out", (B * C, L), F32, kind="ExternalOutput").ap()
    build(nc, *args, res)
    r = run_bass_kernel_spmd(nc, [arrays], core_ids=[0])
    return r.results[0]["out"].reshape(_OUT)
```
